# Optimizing a Trainium2 kernel written in Bass

```python
import numpy as np
import jax
import jax.numpy as jnp

def _softmax(x, axis=-1):
    return jax.nn.softmax(x, axis=axis)

def _gelu(x):
    return jax.nn.gelu(x, approximate=True)

def _silu(x):
    return jax.nn.silu(x)

def _sigmoid(x):
    return jax.nn.sigmoid(x)

def _layernorm(x, axis=-1, eps=1e-05):
    m = jnp.mean(x, axis=axis, keepdims=True)
    v = jnp.var(x, axis=axis, keepdims=True)
    return (x - m) / jnp.sqrt(v + eps)

def _scatter_add(tgt, idx, src, axis=0):
    return tgt.at[idx].add(src)

def _segment_sum(src, seg, n):
    return jax.ops.segment_sum(src, seg, n)
kernel_name = 'mk_xattn_ffn_d2_seqx_r8_af9b7c'

def setup_inputs(seed: int=0):
    np.random.seed(seed)
    _w = jnp.asarray

    def _rec_inputs():
        import jax
        import jax.numpy as jnp
        _rk = jax.random.key(seed)
        x = -0.0002928 + 1 * jax.random.normal(jax.random.fold_in(_rk, 1), (8, 256, 128), jnp.float32)
        _lenS = 256 - jax.random.randint(jax.random.fold_in(_rk, 7), (8,), 0, max(1, 256 // 4) + 1, jnp.int32)
        _lenS2 = 256 - jax.random.randint(jax.random.fold_in(_rk, 8), (8,), 0, max(1, 256 // 4) + 1, jnp.int32)
        _ctx_512P = jax.random.normal(jax.random.fold_in(_rk, 11), (8, 16, 64), jnp.float32)
        _ctx_512c = jax.random.dirichlet(jax.random.fold_in(_rk, 511), 0.3 * jnp.ones((16,), jnp.float32), (8, 256))
        _ctx_512t = jnp.einsum('bsk,bkd->bsd', _ctx_512c, _ctx_512P)
        _ctx_512t = _ctx_512t * jax.lax.rsqrt(jnp.mean(jnp.square(_ctx_512t)) + 1e-12) * 0.953939
        ctx_512 = 0.00222621 + 0.99962 * (_ctx_512t + 0.3 * jax.random.normal(jax.random.fold_in(_rk, 611), (8, 256, 64), jnp.float32))
        return (x, ctx_512)
    x, ctx_512 = _rec_inputs()

    def _L0_xattn_setup():
        import jax, jax.numpy as jnp
        import numpy as np
        B, T, TC, C, CC, H = (2, 256, 64, 128, 64, 16)
        D = C // H

        def _heads(t):
            b, l, _ = t.shape
            return t.reshape(b, l, H, D).transpose(0, 2, 1, 3)
        key = jax.random.key(seed)
        ks = jax.random.split(key, 18)
        w = lambda k, i, o: jax.random.normal(k, (i, o), jnp.float32) / np.sqrt(i).astype(np.float32)
        return {'x': jax.random.normal(ks[0], (B, T, C), jnp.float32), 'cross_input': jax.random.normal(ks[1], (B, TC, CC), jnp.float32), 'Wk': w(ks[2], C, C), 'bk': jnp.zeros((C,), jnp.float32), 'Wq': w(ks[3], C, C), 'bq': jnp.zeros((C,), jnp.float32), 'Wv': w(ks[4], C, C), 'bv': jnp.zeros((C,), jnp.float32), 'Wck': w(ks[5], CC, C), 'bck': jnp.zeros((C,), jnp.float32), 'Wcq': w(ks[6], C, C), 'bcq': jnp.zeros((C,), jnp.float32), 'Wcv': w(ks[7], CC, C), 'bcv': jnp.zeros((C,), jnp.float32), 'Wp': w(ks[8], C, C), 'bp': jnp.zeros((C,), jnp.float32)}
    _L0_xattn_all = _L0_xattn_setup()
    _L0_xattn_in = {k: v for k, v in _L0_xattn_all.items() if k in ('Wk', 'bk', 'Wq', 'bq', 'Wv', 'bv', 'Wck', 'bck', 'Wcq', 'bcq', 'Wcv', 'bcv', 'Wp', 'bp')}
    del _L0_xattn_all

    def _L0_ffn_setup():
        import jax, jax.numpy as jnp
        import numpy as np
        B, L, D = (2, 256, 128)
        E = 15
        H = D * 1
        K = 3
        T = 1.0
        key = jax.random.key(seed)
        ks = jax.random.split(key, 12)
        s = 0.02
        return {'x': jax.random.normal(ks[0], (B, L, D), dtype=jnp.float32), 'router_W': jax.random.normal(ks[1], (D, E), dtype=jnp.float32) * s, 'router_b': jnp.zeros((E,), dtype=jnp.float32), 'sW1': jax.random.normal(ks[2], (D, H), dtype=jnp.float32) * s, 'sb1': jnp.zeros((H,), dtype=jnp.float32), 'sW2': jax.random.normal(ks[3], (H, D), dtype=jnp.float32) * s, 'sb2': jnp.zeros((D,), dtype=jnp.float32), 'eW1': jax.random.normal(ks[4], (E, D, H), dtype=jnp.float32) * s, 'eb1': jnp.zeros((E, H), dtype=jnp.float32), 'eW2': jax.random.normal(ks[5], (E, H, D), dtype=jnp.float32) * s, 'eb2': jnp.zeros((E, D), dtype=jnp.float32)}
    _L0_ffn_all = _L0_ffn_setup()
    _L0_ffn_in = {k: v for k, v in _L0_ffn_all.items() if k in ('router_W', 'router_b', 'sW1', 'sb1', 'sW2', 'sb2', 'eW1', 'eb1', 'eW2', 'eb2')}
    del _L0_ffn_all

    def _L1_xattn_setup():
        import jax, jax.numpy as jnp
        import numpy as np
        H, D, C1, C2, S, M, B, W = (16, 32, 128, 64, 256, 64, 2, 4)

        def _ln(x, g, b):
            m = jnp.mean(x, -1, keepdims=True)
            v = jnp.var(x, -1, keepdims=True)
            return (x - m) * jax.lax.rsqrt(v + 1e-05) * g + b

        def _mha(x, y, wq, wk, wv, li1_w, li1_b, lnx_g, lnx_b, lny_g, lny_b, ln3_g, ln3_b, li2_w, li2_b, li3_w, li3_b, causal):
            xn = _ln(x, lnx_g, lnx_b)
            yn = _ln(y, lny_g, lny_b)
            q = jnp.einsum('bsc,hcd->bhsd', xn, wq)
            k = jnp.einsum('btc,hcd->bhtd', yn, wk)
            v = jnp.einsum('btc,hcd->bhtd', yn, wv)
            a = jax.nn.softmax(jnp.einsum('bhsd,bhtd->bhst', q, k) * D ** (-0.5), axis=-1)
            if causal:
                s, t = (a.shape[-2], a.shape[-1])
                mask = (jnp.arange(t)[None, :] > jnp.arange(s)[:, None]).astype(a.dtype)
                a = a * mask
            o = jnp.einsum('bhst,bhtd->bhsd', a, v)
            o = o.transpose(0, 2, 1, 3).reshape(x.shape[0], x.shape[1], H * D)
            x_out = x + o @ li1_w + li1_b
            h = jax.nn.gelu(_ln(x_out, ln3_g, ln3_b) @ li2_w + li2_b, approximate=False)
            return x_out + h @ li3_w + li3_b
        key = jax.random.key(seed)
        ks = iter(jax.random.split(key, 64))

        def w(shape, scale=0.02):
            return jax.random.normal(next(ks), shape, jnp.float32) * scale
        inp = {'xx': jax.random.normal(next(ks), (B, S, C1), jnp.float32), 'ee': jax.random.normal(next(ks), (B, M, C2), jnp.float32), 'ln1_g': jnp.ones(C1, jnp.float32), 'ln1_b': jnp.zeros(C1, jnp.float32), 'ln2_g': jnp.ones(C1, jnp.float32), 'ln2_b': jnp.zeros(C1, jnp.float32)}
        for pfx, cy in (('a1', C1), ('a2', C2)):
            inp[pfx + '_wq'] = w((H, C1, D))
            inp[pfx + '_wk'] = w((H, cy, D))
            inp[pfx + '_wv'] = w((H, cy, D))
            inp[pfx + '_li1_w'] = w((H * D, C1))
            inp[pfx + '_li1_b'] = jnp.zeros(C1, jnp.float32)
            inp[pfx + '_lnx_g'] = jnp.ones(C1, jnp.float32)
            inp[pfx + '_lnx_b'] = jnp.zeros(C1, jnp.float32)
            inp[pfx + '_lny_g'] = jnp.ones(cy, jnp.float32)
            inp[pfx + '_lny_b'] = jnp.zeros(cy, jnp.float32)
            inp[pfx + '_ln3_g'] = jnp.ones(C1, jnp.float32)
            inp[pfx + '_ln3_b'] = jnp.zeros(C1, jnp.float32)
            inp[pfx + '_li2_w'] = w((C1, C1 * W))
            inp[pfx + '_li2_b'] = jnp.zeros(C1 * W, jnp.float32)
            inp[pfx + '_li3_w'] = w((C1 * W, C1))
            inp[pfx + '_li3_b'] = jnp.zeros(C1, jnp.float32)
        inp['training'] = 0
        return inp
    _L1_xattn_all = _L1_xattn_setup()
    _L1_xattn_in = {k: v for k, v in _L1_xattn_all.items() if k in ('ln1_g', 'ln1_b', 'ln2_g', 'ln2_b', 'a1_wq', 'a1_wk', 'a1_wv', 'a1_li1_w', 'a1_li1_b', 'a1_lnx_g', 'a1_lnx_b', 'a1_lny_g', 'a1_lny_b', 'a1_ln3_g', 'a1_ln3_b', 'a1_li2_w', 'a1_li2_b', 'a1_li3_w', 'a1_li3_b', 'a2_wq', 'a2_wk', 'a2_wv', 'a2_li1_w', 'a2_li1_b', 'a2_lnx_g', 'a2_lnx_b', 'a2_lny_g', 'a2_lny_b', 'a2_ln3_g', 'a2_ln3_b', 'a2_li2_w', 'a2_li2_b', 'a2_li3_w', 'a2_li3_b')}
    del _L1_xattn_all

    def _L1_ffn_setup():
        import jax, jax.numpy as jnp
        import numpy as np
        B, S, D = (4, 64, 128)
        E, K, H = (64, 8, 32)
        ES, HS = (2, 256)
        key = jax.random.key(seed)
        ks = jax.random.split(key, 8)
        scale = 0.02
        rn = lambda k, shape, s: jax.random.normal(k, shape, jnp.float32) * s
        return {'x': rn(ks[0], (B, S, D), 1.0), 'router_w': rn(ks[1], (D, E), scale), 'router_b': jnp.zeros((E,), jnp.float32), 'w1': rn(ks[2], (E, D, H), scale), 'b1': jnp.zeros((E, H), jnp.float32), 'w2': rn(ks[3], (E, H, D), scale), 'b2': jnp.zeros((E, D), jnp.float32), 'sw1': rn(ks[4], (ES, D, HS), scale), 'sb1': jnp.zeros((ES, HS), jnp.float32), 'sw2': rn(ks[5], (ES, HS, D), scale), 'sb2': jnp.zeros((ES, D), jnp.float32)}
    _L1_ffn_all = _L1_ffn_setup()
    _L1_ffn_in = {k: v for k, v in _L1_ffn_all.items() if k in ('router_w', 'router_b', 'w1', 'b1', 'w2', 'b2', 'sw1', 'sb1', 'sw2', 'sb2')}
    del _L1_ffn_all
    return {'x': x, 'ctx_512': ctx_512, 'L0_xattn_Wk': _L0_xattn_in['Wk'], 'L0_xattn_bk': _L0_xattn_in['bk'], 'L0_xattn_Wq': _L0_xattn_in['Wq'], 'L0_xattn_bq': _L0_xattn_in['bq'], 'L0_xattn_Wv': _L0_xattn_in['Wv'], 'L0_xattn_bv': _L0_xattn_in['bv'], 'L0_xattn_Wck': _L0_xattn_in['Wck'], 'L0_xattn_bck': _L0_xattn_in['bck'], 'L0_xattn_Wcq': _L0_xattn_in['Wcq'], 'L0_xattn_bcq': _L0_xattn_in['bcq'], 'L0_xattn_Wcv': _L0_xattn_in['Wcv'], 'L0_xattn_bcv': _L0_xattn_in['bcv'], 'L0_xattn_Wp': _L0_xattn_in['Wp'], 'L0_xattn_bp': _L0_xattn_in['bp'], 'L0_ffn_router_W': _L0_ffn_in['router_W'], 'L0_ffn_router_b': _L0_ffn_in['router_b'], 'L0_ffn_sW1': _L0_ffn_in['sW1'], 'L0_ffn_sb1': _L0_ffn_in['sb1'], 'L0_ffn_sW2': _L0_ffn_in['sW2'], 'L0_ffn_sb2': _L0_ffn_in['sb2'], 'L0_ffn_eW1': _L0_ffn_in['eW1'], 'L0_ffn_eb1': _L0_ffn_in['eb1'], 'L0_ffn_eW2': _L0_ffn_in['eW2'], 'L0_ffn_eb2': _L0_ffn_in['eb2'], 'L1_xattn_ln1_g': _L1_xattn_in['ln1_g'], 'L1_xattn_ln1_b': _L1_xattn_in['ln1_b'], 'L1_xattn_ln2_g': _L1_xattn_in['ln2_g'], 'L1_xattn_ln2_b': _L1_xattn_in['ln2_b'], 'L1_xattn_a1_wq': _L1_xattn_in['a1_wq'], 'L1_xattn_a1_wk': _L1_xattn_in['a1_wk'], 'L1_xattn_a1_wv': _L1_xattn_in['a1_wv'], 'L1_xattn_a1_li1_w': _L1_xattn_in['a1_li1_w'], 'L1_xattn_a1_li1_b': _L1_xattn_in['a1_li1_b'], 'L1_xattn_a1_lnx_g': _L1_xattn_in['a1_lnx_g'], 'L1_xattn_a1_lnx_b': _L1_xattn_in['a1_lnx_b'], 'L1_xattn_a1_lny_g': _L1_xattn_in['a1_lny_g'], 'L1_xattn_a1_lny_b': _L1_xattn_in['a1_lny_b'], 'L1_xattn_a1_ln3_g': _L1_xattn_in['a1_ln3_g'], 'L1_xattn_a1_ln3_b': _L1_xattn_in['a1_ln3_b'], 'L1_xattn_a1_li2_w': _L1_xattn_in['a1_li2_w'], 'L1_xattn_a1_li2_b': _L1_xattn_in['a1_li2_b'], 'L1_xattn_a1_li3_w': _L1_xattn_in['a1_li3_w'], 'L1_xattn_a1_li3_b': _L1_xattn_in['a1_li3_b'], 'L1_xattn_a2_wq': _L1_xattn_in['a2_wq'], 'L1_xattn_a2_wk': _L1_xattn_in['a2_wk'], 'L1_xattn_a2_wv': _L1_xattn_in['a2_wv'], 'L1_xattn_a2_li1_w': _L1_xattn_in['a2_li1_w'], 'L1_xattn_a2_li1_b': _L1_xattn_in['a2_li1_b'], 'L1_xattn_a2_lnx_g': _L1_xattn_in['a2_lnx_g'], 'L1_xattn_a2_lnx_b': _L1_xattn_in['a2_lnx_b'], 'L1_xattn_a2_lny_g': _L1_xattn_in['a2_lny_g'], 'L1_xattn_a2_lny_b': _L1_xattn_in['a2_lny_b'], 'L1_xattn_a2_ln3_g': _L1_xattn_in['a2_ln3_g'], 'L1_xattn_a2_ln3_b': _L1_xattn_in['a2_ln3_b'], 'L1_xattn_a2_li2_w': _L1_xattn_in['a2_li2_w'], 'L1_xattn_a2_li2_b': _L1_xattn_in['a2_li2_b'], 'L1_xattn_a2_li3_w': _L1_xattn_in['a2_li3_w'], 'L1_xattn_a2_li3_b': _L1_xattn_in['a2_li3_b'], 'L1_ffn_router_w': _L1_ffn_in['router_w'], 'L1_ffn_router_b': _L1_ffn_in['router_b'], 'L1_ffn_w1': _L1_ffn_in['w1'], 'L1_ffn_b1': _L1_ffn_in['b1'], 'L1_ffn_w2': _L1_ffn_in['w2'], 'L1_ffn_b2': _L1_ffn_in['b2'], 'L1_ffn_sw1': _L1_ffn_in['sw1'], 'L1_ffn_sb1': _L1_ffn_in['sb1'], 'L1_ffn_sw2': _L1_ffn_in['sw2'], 'L1_ffn_sb2': _L1_ffn_in['sb2']}

def reference(x, ctx_512, L0_xattn_Wk, L0_xattn_bk, L0_xattn_Wq, L0_xattn_bq, L0_xattn_Wv, L0_xattn_bv, L0_xattn_Wck, L0_xattn_bck, L0_xattn_Wcq, L0_xattn_bcq, L0_xattn_Wcv, L0_xattn_bcv, L0_xattn_Wp, L0_xattn_bp, L0_ffn_router_W, L0_ffn_router_b, L0_ffn_sW1, L0_ffn_sb1, L0_ffn_sW2, L0_ffn_sb2, L0_ffn_eW1, L0_ffn_eb1, L0_ffn_eW2, L0_ffn_eb2, L1_xattn_ln1_g, L1_xattn_ln1_b, L1_xattn_ln2_g, L1_xattn_ln2_b, L1_xattn_a1_wq, L1_xattn_a1_wk, L1_xattn_a1_wv, L1_xattn_a1_li1_w, L1_xattn_a1_li1_b, L1_xattn_a1_lnx_g, L1_xattn_a1_lnx_b, L1_xattn_a1_lny_g, L1_xattn_a1_lny_b, L1_xattn_a1_ln3_g, L1_xattn_a1_ln3_b, L1_xattn_a1_li2_w, L1_xattn_a1_li2_b, L1_xattn_a1_li3_w, L1_xattn_a1_li3_b, L1_xattn_a2_wq, L1_xattn_a2_wk, L1_xattn_a2_wv, L1_xattn_a2_li1_w, L1_xattn_a2_li1_b, L1_xattn_a2_lnx_g, L1_xattn_a2_lnx_b, L1_xattn_a2_lny_g, L1_xattn_a2_lny_b, L1_xattn_a2_ln3_g, L1_xattn_a2_ln3_b, L1_xattn_a2_li2_w, L1_xattn_a2_li2_b, L1_xattn_a2_li3_w, L1_xattn_a2_li3_b, L1_ffn_router_w, L1_ffn_router_b, L1_ffn_w1, L1_ffn_b1, L1_ffn_w2, L1_ffn_b2, L1_ffn_sw1, L1_ffn_sb1, L1_ffn_sw2, L1_ffn_sb2):
    import jax
    import jax.numpy as jnp

    def _L0_xattn_ref(x, cross_input, Wk, bk, Wq, bq, Wv, bv, Wck, bck, Wcq, bcq, Wcv, bcv, Wp, bp):
        import jax, jax.numpy as jnp
        import numpy as np
        B, T, TC, C, CC, H = (2, 256, 64, 128, 64, 16)
        D = C // H

        def _heads(t):
            b, l, _ = t.shape
            return t.reshape(b, l, H, D).transpose(0, 2, 1, 3)
        scale = np.float32(1.0 / np.sqrt(D))
        q = _heads(x @ Wq + bq)
        k = _heads(x @ Wk + bk)
        v = _heads(x @ Wv + bv)
        att = jnp.einsum('bhqd,bhkd->bhqk', q, k) * scale
        causal = jnp.tril(jnp.ones((T, T), bool))
        att = jnp.where(causal[None, None], att, -jnp.inf)
        y = jnp.einsum('bhqk,bhkd->bhqd', jax.nn.softmax(att, axis=-1), v)
        qc = _heads(x @ Wcq + bcq)
        kc = _heads(cross_input @ Wck + bck)
        vc = _heads(cross_input @ Wcv + bcv)
        attc = jnp.einsum('bhqd,bhkd->bhqk', qc, kc) * scale
        y = y + jnp.einsum('bhqk,bhkd->bhqd', jax.nn.softmax(attc, axis=-1), vc)
        y = y.transpose(0, 2, 1, 3).reshape(x.shape[0], T, C)
        return y @ Wp + bp

    def _L0_ffn_ref(x, router_W, router_b, sW1, sb1, sW2, sb2, eW1, eb1, eW2, eb2):
        import jax, jax.numpy as jnp
        import numpy as np
        B, L, D = (2, 256, 128)
        E = 15
        H = D * 1
        K = 3
        T = 1.0
        b, l, d = x.shape
        n = b * l
        xt = x.reshape(n, d)
        shared = jax.nn.relu(xt @ sW1 + sb1) @ sW2 + sb2
        logits = xt @ router_W + router_b
        probs = jax.nn.softmax(logits / T, axis=-1)
        top_p, top_i = jax.lax.top_k(probs, K)
        cw = jnp.zeros((n, E), dtype=probs.dtype)
        cw = cw.at[jnp.arange(n)[:, None], top_i].set(top_p)
        h = jax.nn.relu(jnp.einsum('nd,edh->neh', xt, eW1) + eb1)
        ye = jnp.einsum('neh,ehd->ned', h, eW2) + eb2
        routed = jnp.einsum('ned,ne->nd', ye, cw)
        return (shared + routed).reshape(b, l, d)

    def _L1_xattn_ref(xx, ee, ln1_g, ln1_b, ln2_g, ln2_b, a1_wq, a1_wk, a1_wv, a1_li1_w, a1_li1_b, a1_lnx_g, a1_lnx_b, a1_lny_g, a1_lny_b, a1_ln3_g, a1_ln3_b, a1_li2_w, a1_li2_b, a1_li3_w, a1_li3_b, a2_wq, a2_wk, a2_wv, a2_li1_w, a2_li1_b, a2_lnx_g, a2_lnx_b, a2_lny_g, a2_lny_b, a2_ln3_g, a2_ln3_b, a2_li2_w, a2_li2_b, a2_li3_w, a2_li3_b, training):
        import jax, jax.numpy as jnp
        import numpy as np
        H, D, C1, C2, S, M, B, W = (16, 32, 128, 64, 256, 64, 2, 4)

        def _ln(x, g, b):
            m = jnp.mean(x, -1, keepdims=True)
            v = jnp.var(x, -1, keepdims=True)
            return (x - m) * jax.lax.rsqrt(v + 1e-05) * g + b

        def _mha(x, y, wq, wk, wv, li1_w, li1_b, lnx_g, lnx_b, lny_g, lny_b, ln3_g, ln3_b, li2_w, li2_b, li3_w, li3_b, causal):
            xn = _ln(x, lnx_g, lnx_b)
            yn = _ln(y, lny_g, lny_b)
            q = jnp.einsum('bsc,hcd->bhsd', xn, wq)
            k = jnp.einsum('btc,hcd->bhtd', yn, wk)
            v = jnp.einsum('btc,hcd->bhtd', yn, wv)
            a = jax.nn.softmax(jnp.einsum('bhsd,bhtd->bhst', q, k) * D ** (-0.5), axis=-1)
            if causal:
                s, t = (a.shape[-2], a.shape[-1])
                mask = (jnp.arange(t)[None, :] > jnp.arange(s)[:, None]).astype(a.dtype)
                a = a * mask
            o = jnp.einsum('bhst,bhtd->bhsd', a, v)
            o = o.transpose(0, 2, 1, 3).reshape(x.shape[0], x.shape[1], H * D)
            x_out = x + o @ li1_w + li1_b
            h = jax.nn.gelu(_ln(x_out, ln3_g, ln3_b) @ li2_w + li2_b, approximate=False)
            return x_out + h @ li3_w + li3_b
        x = _ln(xx, ln1_g, ln1_b)
        x = x + _mha(x, x, a1_wq, a1_wk, a1_wv, a1_li1_w, a1_li1_b, a1_lnx_g, a1_lnx_b, a1_lny_g, a1_lny_b, a1_ln3_g, a1_ln3_b, a1_li2_w, a1_li2_b, a1_li3_w, a1_li3_b, causal=True)
        x = _ln(x, ln2_g, ln2_b)
        return x + _mha(x, ee, a2_wq, a2_wk, a2_wv, a2_li1_w, a2_li1_b, a2_lnx_g, a2_lnx_b, a2_lny_g, a2_lny_b, a2_ln3_g, a2_ln3_b, a2_li2_w, a2_li2_b, a2_li3_w, a2_li3_b, causal=False)

    def _L1_ffn_ref(x, router_w, router_b, w1, b1, w2, b2, sw1, sb1, sw2, sb2):
        import jax, jax.numpy as jnp
        import numpy as np
        B, S, D = (4, 64, 128)
        E, K, H = (64, 8, 32)
        ES, HS = (2, 256)
        b_, s_, d_ = x.shape
        xf = x.reshape(-1, d_)
        probs = jax.nn.softmax(xf @ router_w + router_b, axis=-1)
        tw, ti = jax.lax.top_k(probs, K)
        tw = tw / jnp.sum(tw, axis=-1, keepdims=True)

        def body(acc, p):
            W1, B1, W2, B2, e = p
            h = jax.nn.silu(xf @ W1 + B1) @ W2 + B2
            cw = jnp.sum(jnp.where(ti == e, tw, 0.0), axis=-1)
            return (acc + cw[:, None] * h, None)
        routed, _ = jax.lax.scan(body, jnp.zeros_like(xf), (w1, b1, w2, b2, jnp.arange(w1.shape[0])))

        def shared_mlp(W1, B1, W2, B2):
            return jax.nn.silu(xf @ W1 + B1) @ W2 + B2
        shared = jnp.sum(jax.vmap(shared_mlp)(sw1, sb1, sw2, sb2), axis=0)
        return (routed + shared).reshape(b_, s_, d_)
    x = x + _L0_xattn_ref(_layernorm(x, axis=-1), ctx_512, L0_xattn_Wk, L0_xattn_bk, L0_xattn_Wq, L0_xattn_bq, L0_xattn_Wv, L0_xattn_bv, L0_xattn_Wck, L0_xattn_bck, L0_xattn_Wcq, L0_xattn_bcq, L0_xattn_Wcv, L0_xattn_bcv, L0_xattn_Wp, L0_xattn_bp)
    x = x + _L0_ffn_ref(_layernorm(x, axis=-1), L0_ffn_router_W, L0_ffn_router_b, L0_ffn_sW1, L0_ffn_sb1, L0_ffn_sW2, L0_ffn_sb2, L0_ffn_eW1, L0_ffn_eb1, L0_ffn_eW2, L0_ffn_eb2)
    x = x + _L1_xattn_ref(_layernorm(x, axis=-1), ctx_512, L1_xattn_ln1_g, L1_xattn_ln1_b, L1_xattn_ln2_g, L1_xattn_ln2_b, L1_xattn_a1_wq, L1_xattn_a1_wk, L1_xattn_a1_wv, L1_xattn_a1_li1_w, L1_xattn_a1_li1_b, L1_xattn_a1_lnx_g, L1_xattn_a1_lnx_b, L1_xattn_a1_lny_g, L1_xattn_a1_lny_b, L1_xattn_a1_ln3_g, L1_xattn_a1_ln3_b, L1_xattn_a1_li2_w, L1_xattn_a1_li2_b, L1_xattn_a1_li3_w, L1_xattn_a1_li3_b, L1_xattn_a2_wq, L1_xattn_a2_wk, L1_xattn_a2_wv, L1_xattn_a2_li1_w, L1_xattn_a2_li1_b, L1_xattn_a2_lnx_g, L1_xattn_a2_lnx_b, L1_xattn_a2_lny_g, L1_xattn_a2_lny_b, L1_xattn_a2_ln3_g, L1_xattn_a2_ln3_b, L1_xattn_a2_li2_w, L1_xattn_a2_li2_b, L1_xattn_a2_li3_w, L1_xattn_a2_li3_b, 0)
    x = x + _L1_ffn_ref(_layernorm(x, axis=-1), L1_ffn_router_w, L1_ffn_router_b, L1_ffn_w1, L1_ffn_b1, L1_ffn_w2, L1_ffn_b2, L1_ffn_sw1, L1_ffn_sb1, L1_ffn_sw2, L1_ffn_sb2)
    return x

_drawn_inputs = setup_inputs


def setup_inputs(seed=0):
    import zlib

    import numpy as np

    out = dict(_drawn_inputs(seed))
    spreads = {'L0_xattn_bk': (0.0, 2.0),
     'L0_xattn_bq': (0.0, 0.457),
     'L0_xattn_bv': (0.0, 0.1),
     'L0_xattn_bck': (0.0, 2.0),
     'L0_xattn_bcq': (0.0, 0.388),
     'L0_xattn_bcv': (0.0, 0.1),
     'L0_xattn_bp': (0.0, 0.1),
     'L0_ffn_router_b': (0.0, 0.8),
     'L0_ffn_sb1': (0.0, 0.668),
     'L0_ffn_sb2': (0.0, 0.1),
     'L0_ffn_eb1': (0.0, 0.8),
     'L0_ffn_eb2': (0.0, 0.612),
     'L1_xattn_ln1_g': (1.0, 0.2),
     'L1_xattn_ln1_b': (0.0, 0.1),
     'L1_xattn_ln2_g': (1.0, 0.2),
     'L1_xattn_ln2_b': (0.0, 0.1),
     'L1_xattn_a1_li1_b': (0.0, 0.43),
     'L1_xattn_a1_lnx_g': (1.0, 0.6),
     'L1_xattn_a1_lnx_b': (0.0, 0.8),
     'L1_xattn_a1_lny_g': (1.0, 0.6),
     'L1_xattn_a1_lny_b': (0.0, 0.8),
     'L1_xattn_a1_ln3_g': (1.0, 0.6),
     'L1_xattn_a1_ln3_b': (0.0, 0.8),
     'L1_xattn_a1_li2_b': (0.0, 0.8),
     'L1_xattn_a1_li3_b': (0.0, 0.451),
     'L1_xattn_a2_li1_b': (0.0, 0.277),
     'L1_xattn_a2_lnx_g': (1.0, 0.6),
     'L1_xattn_a2_lnx_b': (0.0, 0.8),
     'L1_xattn_a2_lny_g': (1.0, 0.6),
     'L1_xattn_a2_lny_b': (0.0, 0.8),
     'L1_xattn_a2_ln3_g': (1.0, 0.6),
     'L1_xattn_a2_ln3_b': (0.0, 0.8),
     'L1_xattn_a2_li2_b': (0.0, 0.8),
     'L1_xattn_a2_li3_b': (0.0, 0.307),
     'L1_ffn_router_b': (0.0, 0.8),
     'L1_ffn_b1': (0.0, 0.8),
     'L1_ffn_b2': (0.0, 0.695),
     'L1_ffn_sb1': (0.0, 0.8),
     'L1_ffn_sb2': (0.0, 0.1)}
    factors = {'L0_ffn_router_W': 4.437,
     'L0_ffn_eW1': 8.0,
     'L0_ffn_eW2': 8.0,
     'L1_xattn_a1_wq': 8.0,
     'L1_xattn_a1_wk': 8.0,
     'L1_xattn_a1_wv': 6.648,
     'L1_xattn_a1_li1_w': 6.235,
     'L1_xattn_a1_li2_w': 3.448,
     'L1_xattn_a1_li3_w': 3.143,
     'L1_xattn_a2_wq': 8.0,
     'L1_xattn_a2_wk': 8.0,
     'L1_xattn_a2_wv': 4.251,
     'L1_xattn_a2_li1_w': 4.346,
     'L1_xattn_a2_li2_w': 3.219,
     'L1_xattn_a2_li3_w': 2.907,
     'L1_ffn_router_w': 5.676,
     'L1_ffn_w1': 8.0,
     'L1_ffn_w2': 8.0,
     'L1_ffn_sw1': 3.422,
     'L1_ffn_sw2': 3.131}
    for name, (base, spread) in spreads.items():
        noise = np.random.default_rng([zlib.crc32(name.encode()), seed]).standard_normal(out[name].shape)
        drawn = base * np.exp(spread * noise) if base else spread * noise
        out[name] = jnp.asarray(drawn.astype(out[name].dtype))
    for name, factor in factors.items():
        out[name] = (out[name] * factor).astype(out[name].dtype)
    return out
```

```python
from contextlib import ExitStack

import numpy as np

import concourse.bass as bass
from concourse import mybir

F32 = mybir.dt.float32
F32R = mybir.dt.float32r
BF16 = mybir.dt.bfloat16
ALU = mybir.AluOpType
ACT = mybir.ActivationFunctionType
AX = mybir.AxisListType

P = 128
NB = 8
S = 256
T = S // P
C = 128
CC = 64
H = 16
HR = 32
NC = H * HR // P
D0, D1 = 8, 32
E0, K0 = 15, 3
E1, K1 = 64, 8
NE0 = E0 + 1
NR1 = E1 * 32 // P
NE1 = NR1 + 2 * 256 // P
EPS = 1e-5
NEG = -1e30
SENT = -2e30
TAKEN = -3e30
RING = 3
PR = 5
PIECES = 4
KROWS = 3 * HR
MROW = KROWS
LPAD = 20


def columns():
    at, out = 0, {}
    for name, n in [
        ("wq0", 128), ("wk0", 128), ("wv0", 512), ("bq0", 4), ("bk0", 4), ("bv0", 4),
        ("wq1", 128), ("wk1", 128), ("wv1", 512), ("bq1", 4), ("bk1", 4), ("bv1", 4),
        ("wp", 512), ("bp", 1), ("rw0", E0), ("rb0", E0), ("eb1", NE0), ("eb2", C), ("sb2", 1),
        ("L1", 0),
        ("wq2", 512), ("wk2", 512), ("wv2", 512), ("li1_2", 512), ("li2_2", 512), ("li3_2", 512),
        ("wq3", 512), ("wk3", 512), ("wv3", 512), ("li1_3", 512), ("li2_3", 512), ("li3_3", 512),
        ("li1b_2", 1), ("li2b_2", 4), ("li3b_2", 1), ("li1b_3", 1), ("li2b_3", 4), ("li3b_3", 1),
        ("gx_2", 1), ("bx_2", 1), ("gy_2", 1), ("by_2", 1), ("g3_2", 1), ("b3_2", 1),
        ("gx_3", 1), ("bx_3", 1), ("gy_3", 1), ("by_3", 1), ("g3_3", 1), ("b3_3", 1),
        ("ln1g", C), ("ln1b", C), ("ln2g", C), ("ln2b", C),
        ("rw1", E1), ("rb1", E1), ("fb1", NE1), ("fb2", C), ("fsb2", 2),
    ]:
        out[name] = (at, n)
        at += n
    return out, at


COLS, NCOLS = columns()


def phase_steps(ph):
    def attention(a):
        yield "project_q", (a,), 4, 1.8
        yield "project_v", (a,), 2, 1.8
        yield "project_k", (a,), 4, 1.8
        yield "wait", (), 0, 10.0
        for h in range(H):
            yield "scores_a", (a, h), 1, 0.6
        yield "wait", (), 0, 0.5
        yield "max_rows", (a,), 1, 4.0
        for h in range(H):
            yield "scores_b", (a, h), 1, 0.5
            if h >= PR - 1 and (h - PR + 1) % 4 == 0:
                yield "values", (a, (h - PR + 1) // 4), 1, 2.2
        yield "values", (a, NC - 1), 1, 2.2
        yield "sums", (a,), 0, 2.0
        yield "normalize", (a,), NC, 1.8

    def back(n):
        yield "back", (n,), 1, 1.2

    def norm(i):
        yield "ln_stats", (i,), 0, 1.5
        yield "ln_apply", (i,), 0, 1.0

    if ph == 0:
        yield "load", (), 0, 2.0
        yield from norm(0)
        yield "turn", (0,), 1, 0.8
        yield "turn_context", (1,), 1, 0.8
        yield from attention(0)
        yield from attention(1)
        yield "out_project", (0, 0), 1, 2.2
        yield from back(0)
        yield from norm(1)
        yield "turn", (2,), 1, 0.8
        yield "router", (), 1, 6.0
        yield "turn_weights", (), 1, 1.0
        for e in range(NE0):
            yield "expert", (e,), 2 if e < E0 else 1, 1.0
        yield "expert_last", (1,), 0, 1.5
        yield from back(1)
    else:
        yield "load", (), 0, 0.0
        yield "take", (), 0, 0.5
        yield from norm(0)
        yield from norm(1)
        yield "affine", (0,), 0, 2.0
        yield from norm(2)
        yield "turn_two", (0,), 1, 1.0
        yield from attention(2)
        yield "out_project", (2, 0), 1, 2.2
        yield from back(0)
        yield from norm(3)
        yield "turn", (1,), 1, 1.0
        yield "mlp", (0, 1), 4, 2.5
        yield "mlp_out", (0, 1), 0, 2.5
        yield from back(1)
        yield from norm(4)
        yield "affine", (1,), 0, 2.0
        yield from norm(5)
        yield "turn", (2,), 1, 1.0
        yield from norm(6)
        yield "turn_context", (3,), 1, 1.0
        yield from attention(3)
        yield "out_project", (3, 2), 1, 2.2
        yield from back(2)
        yield from norm(7)
        yield "turn", (4,), 1, 1.0
        yield "mlp", (1, 3), 4, 2.5
        yield "mlp_out", (1, 3), 0, 2.5
        yield from back(3)
        yield from norm(8)
        yield "turn", (5,), 1, 1.0
        yield "router", (), 1, 6.0
        yield "turn_weights", (), 1, 1.0
        for e in range(NE1):
            yield "expert", (e,), 2 if e < NR1 else 1, 1.0
        yield "expert_last", (4,), 0, 1.5
        yield from back(4)
        yield "store", (), 0, 0.0


def numbered(ph):
    out, r = [], 0
    for name, args, uses, weight in phase_steps(ph):
        out.append((name, ph, r, args, weight))
        r += uses
    return out, r


STEPS = [numbered(ph)[0] for ph in (0, 1)]
USES = [numbered(ph)[1] for ph in (0, 1)]


def merged_order():
    total = [sum(s[4] for s in steps) for steps in STEPS]
    at, done, out = [0, 0], [0.0, 0.0], []
    while at[0] < len(STEPS[0]) or at[1] < len(STEPS[1]):
        left = [ph for ph in (0, 1) if at[ph] < len(STEPS[ph])]
        ph = min(left, key=lambda q: done[q] / total[q])
        step = STEPS[ph][at[ph]]
        out.append(step)
        done[ph] += step[4]
        at[ph] += 1
    return out


BOTH = merged_order()


class Batch:

    def __init__(self, i, plus):
        self.i, self.plus = i, plus

    def times(self, n, more):
        return self.plus * n + more if self.i is None else self.i * n + (self.plus * n + more)


class Signal:

    def __init__(self, sem, per):
        self.sem, self.per = sem, per

    def at(self, b, j):
        return b.times(self.per, j)


def build(nc, resident, pieces0, pieces1, x_in, ctx_in, out, dbg=None):
    with ExitStack() as ctx:
        def sb(name, shape, dt=F32):
            return ctx.enter_context(nc.sbuf_tensor("t_" + name, shape, dt))

        W = sb("resident", [P, NCOLS])

        def col(name, i=0, n=None):
            at, width = COLS[name]
            return W[:, at + i:at + i + (width - i if n is None else n)]

        ident = sb("ident", [P, P])
        identb = sb("identb", [P, P], BF16)
        zerosb = sb("zerosb", [P, P], BF16)
        mask_qk = sb("mask_qk", [P, P], BF16)
        mask_kq = sb("mask_kq", [P, P], BF16)
        pick0 = sb("pick0", [P, E0], F32R)
        pick1 = sb("pick1", [P, E1, HR], F32R)
        spread = sb("spread", [P, NC, 4, HR])
        sum_lhs = sb("sum_lhs", [P, NC, HR])
        minus_half = sb("minus_half", [P, T])
        bv_sum = sb("bv_sum", [P, NC])
        fsb2_sum = sb("fsb2_sum", [P, 1])
        b2hi = [sb(f"b2hi{ph}", [P, C], F32R) for ph in (0, 1)]
        b2lo = [sb(f"b2lo{ph}", [P, C], F32R) for ph in (0, 1)]

        def two(name, shape, dt=F32):
            return [sb(f"{name}{ph}", shape, dt) for ph in (0, 1)]

        xin = sb("xin", [P, T, C])
        x1 = sb("x1", [P, T, C])
        handed = sb("handed", [P, T, C])
        X0 = sb("X0", [P, T, C])
        X1 = sb("X1", [P, T, C])
        XO = sb("XO", [P, T, C])
        XS = sb("XS", [P, T, C])
        scaled = sb("scaled", [P, T, C])
        result = sb("result", [P, T, C])
        ctok = two("ctok", [P, T, CC])
        xh = two("xh", [P, T, C])
        stats = two("stats", [P, T, 6])
        mv = two("mv", [P, T, 2])
        ve = two("ve", [P, T])
        rstd = two("rstd", [P, T])
        xT = two("xT", [P, S])
        yT = sb("yT", [P, S])
        cT = two("cT", [P, S])
        O = two("O", [P, NC, S])
        low = two("low", [P, NC, S])
        SH = [O[ph][:, :, :].bitcast(F32R) for ph in (0, 1)]
        SL = [low[ph][:, :, :].bitcast(F32R) for ph in (0, 1)]
        qs = two("qs", [P, H, S], F32R)
        ks = two("ks", [P, H, S], F32R)
        V = two("V", [P, T, H * HR])
        negmax = two("negmax", [P, T, H])
        MH = two("MH", [H, S], F32R)
        ML = two("ML", [H, S], F32R)
        probs = two("probs", [P, PR, 2 * S])
        masked = sb("masked", [P, PR, 2, P])
        Y0 = sb("Y0", [P, NC, S])
        R = two("R", [P, S])
        F = two("F", [P, S])
        hidden = low[1]
        logits = [sb("logits0", [P, T, LPAD]), sb("logits1", [P, T, E1])]
        left = [sb("left0", [P, T, LPAD]), sb("left1", [P, T, E1])]
        top8 = two("top8", [P, T, 8])
        take3 = sb("take3", [P, T, 8])
        nmx = two("nmx", [P, T])
        chosen = [sb("chosen0", [P, T, E0]), sb("chosen1", [P, T, E1])]
        expl = [sb("expl0", [P, T, E0]), sb("expl1", [P, T, E1])]
        esum = two("esum", [P, T])
        cw = [sb("cw0", [P, T, E0]), sb("cw1", [P, T, E1])]
        CS = two("CS", [P, S], F32R)
        late = [low[0], masked[:, :, :, :].rearrange("p a b n -> p a (b n)")]
        Hx = [late[ph][:, 0:2, :] for ph in (0, 1)]
        G = [late[ph][:, 2:4, :] for ph in (0, 1)]
        piece = two("piece", [P, PIECES, 2 * C])

        ring = [[ctx.enter_context(nc.psum_tensor(f"ring{ph}{s}", [P, 512], F32)) for s in range(RING)]
                for ph in (0, 1)]
        acc = [ctx.enter_context(nc.psum_tensor(f"acc{ph}", [P, 512], F32)) for ph in (0, 1)]

        def sem(name):
            return ctx.enter_context(nc.semaphore(name))

        def signals(name, per0, per1):
            return [Signal(sem(f"{name}{ph}") if per else None, per) for ph, per in ((0, per0), (1, per1))]

        s_res = [sem("resident0"), sem("resident1")]
        s_const = sem("constants")
        s_ready = sem("setup_done")
        s_ones = sem("high_parts_of_b2")
        s_passed = sem("passed_waits")
        full = [[Signal(sem(f"full{ph}{s}"), (USES[ph] - s + RING - 1) // RING) for s in range(RING)]
                for ph in (0, 1)]
        free = [[Signal(sem(f"free{ph}{s}"), (USES[ph] - s + RING - 1) // RING) for s in range(RING)]
                for ph in (0, 1)]
        acc_full = signals("acc_full", 3, 5)
        acc_free = signals("acc_free", 3, 5)
        x_loaded = signals("x_loaded", 16, 0)
        c_loaded = signals("c_loaded", 16, 16)
        var_done = signals("var_done", 2, 9)
        rstd_done = signals("rstd_done", 2, 9)
        xh_done = signals("xh_done", 2, 9)
        affine_done = signals("affine_done", 0, 2)
        xT_done = signals("xT_done", 3, 6)
        yT_done = signals("yT_done", 0, 1)
        hi_done = signals("hi_done", 16, 16)
        lo_done = signals("lo_done", 16, 16)
        q_stacked = signals("q_stacked", 2 * 12 * 16, 2 * 12 * 16)
        k_stacked = signals("k_stacked", 2 * 12 * 16, 2 * 12 * 16)
        v_done = signals("v_done", 4, 4)
        max_done = signals("max_done", 32, 32)
        mh_done = signals("mh_done", 2, 2)
        ml_done = signals("ml_done", 2, 2)
        m_stacked = signals("m_stacked", 64, 64)
        exp_done = signals("exp_done", 32, 32)
        masked_done = signals("masked_done", 0, 16)
        o_done = signals("o_done", 8, 8)
        r_done = signals("r_done", 2, 2)
        on_done = signals("on_done", 8, 8)
        f_done = signals("f_done", 2, 5)
        back_done = signals("back_done", 2, 5)
        hidden_done = signals("hidden_done", 0, 8)
        xs_done = signals("xs_done", 0, 2)
        logits_done = signals("logits_done", 1, 1)
        expl_done = signals("expl_done", 1, 1)
        cw_done = signals("cw_done", 1, 1)
        cs_hi = signals("cs_hi", 1, 1)
        cs_lo = signals("cs_lo", 1, 1)
        act_done = signals("act_done", NE0, NE1)
        gated = signals("gated", E0, NR1)
        y_done = signals("y_done", NE0, NE1)
        loaded = [[Signal(sem(f"piece{ph}{s}"), 16 * n // PIECES) for s in range(PIECES)]
                  for ph, n in ((0, NE0), (1, NE1))]
        stored = Signal(sem("stored"), 16)

        dram_x = x_in.rearrange("b (t p) c -> b p t c", p=P)
        dram_c = ctx_in.rearrange("b (t p) c -> b p t c", p=P)
        dram_o = out.rearrange("b (t p) c -> b p t c", p=P)
        pieces = [pieces0, pieces1]
        NEXP = [NE0, NE1]
        NROUTED = [E0, NR1]
        NEXPERTS = [E0, E1]
        DH = [D0, D1]

        def ordinal(ph, a):
            return a - 2 * ph

        def settle(eng):
            eng.sem_inc(s_passed, 1)

        def drive(eng, steps):
            def run(order, b0, b1):
                for name, ph, r, args, _ in order:
                    if name in steps:
                        steps[name](ph, b1 if ph else b0, r, *args)

            run(STEPS[0], Batch(None, 0), None)
            with eng.Fori(0, NB - 1) as i:
                run(BOTH, Batch(i, 1), Batch(i, 0))
            run(STEPS[1], None, Batch(None, NB - 1))

        block = ctx.enter_context(nc.Block())

        @block.sync
        def _(sp):
            l1 = COLS["L1"][0]
            sp.dma_start(W[:, 0:l1], resident[:, 0:l1]).then_inc(s_res[0], 16)
            sp.dma_start(W[:, l1:NCOLS], resident[:, l1:NCOLS]).then_inc(s_res[1], 16)

            def load(ph, b, r):
                i = b.times(1, 0)
                if ph == 0:
                    if b.i is not None:
                        sp.wait_ge(back_done[0].sem, b.times(2, -1))
                        settle(sp)
                    sp.dma_start(xin[:, :, :], dram_x[i]).then_inc(x_loaded[0].sem, 16)
                if ph == 1 and b.plus == NB - 1 or b.i is not None:
                    if ph == 0:
                        sp.wait_ge(xT_done[0].sem, b.times(3, -1))
                    else:
                        sp.wait_ge(stored.sem, b.times(16, 16))
                    settle(sp)
                sp.dma_start(ctok[ph][:, :, :], dram_c[i]).then_inc(c_loaded[ph].sem, 16)

            def stack(ph, b, a, src_done, terms, sig):
                sp.wait_ge(lo_done[ph].sem, lo_done[ph].at(b, 8 * ordinal(ph, a) + src_done))
                d = DH[ph]
                for term, (src, dst) in enumerate(terms):
                    for j in range(4):
                        to = dst[HR * term:HR * term + d, :, :].rearrange("p (c j) n -> p c j n", j=4)[:, :, j, :]
                        sp.dma_start(to.bitcast(F32), src[d * j:d * (j + 1), :, :].bitcast(F32)).then_inc(sig[ph].sem, 16)

            def project_q(ph, b, r, a):
                stack(ph, b, a, 4, [(SH[ph], qs[ph]), (SH[ph], qs[ph]), (SL[ph], qs[ph])], q_stacked)

            def project_k(ph, b, r, a):
                stack(ph, b, a, 8, [(SH[ph], ks[ph]), (SL[ph], ks[ph]), (SH[ph], ks[ph])], k_stacked)

            def max_rows(ph, b, r, a):
                n = ordinal(ph, a) + 1
                for row, tile, done in ((MROW, MH, mh_done), (MROW + 1, ML, ml_done)):
                    sp.wait_ge(done[ph].sem, done[ph].at(b, n))
                    sp.dma_start(qs[ph][row:row + 1, :, :].bitcast(F32), tile[ph][:, :].bitcast(F32)).then_inc(m_stacked[ph].sem, 16)

            def store(ph, b, r):
                sp.wait_ge(back_done[1].sem, back_done[1].at(b, 5))
                settle(sp)
                sp.dma_start(dram_o[b.times(1, 0)], result[:, :, :]).then_inc(stored.sem, 16)
                sp.wait_ge(stored.sem, stored.at(b, 32))
                settle(sp)

            sp.wait_ge(s_res[1], 16)
            sp.sem_inc(stored.sem, 16)
            drive(sp, dict(load=load, project_q=project_q, project_k=project_k, max_rows=max_rows, store=store))

        @block.gpsimd
        def _(pool):
            def select(tile, src, op, fill, base):
                return pool.affine_select(out=tile[:, :], in_=src[:, :], compare_op=op, fill=fill, base=base,
                                          pattern=[[-1, P]], channel_multiplier=1)
            pool.memset(ident[:, :], 0.0)
            pool.memset(zerosb[:, :], 0.0)
            pool.memset(minus_half[:, :], -0.5)
            pool.drain()
            select(ident, ident, ALU.not_equal, 1.0, 0)
            select(mask_qk, zerosb, ALU.is_ge, NEG, 0)
            pool.affine_select(out=mask_kq[:, :], in_=zerosb[:, :], compare_op=ALU.is_ge, fill=NEG, base=0,
                               pattern=[[1, P]], channel_multiplier=-1)
            pool.drain()
            pool.tensor_copy(identb[:, :], ident[:, :]).then_inc(s_const, 1)
            for ph in (0, 1):
                pool.memset(qs[ph][:, :, :].bitcast(F32), 0.0)
                pool.memset(ks[ph][0:KROWS, :, :].bitcast(F32), 0.0)
                pool.drain()
                pool.memset(ks[ph][KROWS:P, :, :].bitcast(F32), 1.0)
                pool.drain()
            for ph in (0, 1):
                pool.memset(CS[ph][:, :].bitcast(F32), 0.0)
                pool.memset(cT[ph][:, :], 0.0)
            pool.drain()
            pool.sem_inc(s_const, 1)
            for ph in (0, 1):
                for e in range(PIECES):
                    pool.dma_start(piece[ph][:, e, :], pieces[ph][e]).then_inc(loaded[ph][e].sem, 16)
            pool.wait_ge(s_res[1], 16)
            pool.wait_ge(s_ready, 2)

            def ln_stats(ph, b, r, i):
                pool.wait_ge(var_done[ph].sem, var_done[ph].at(b, i + 1))
                pool.tensor_tensor(rstd[ph][:, :], ve[ph][:, :], minus_half[:, :], ALU.pow).then_inc(rstd_done[ph].sem, 1)

            def affine(ph, b, r, i):
                g, beta = (("ln1g", "ln1b"), ("ln2g", "ln2b"))[i]
                pool.wait_ge(xh_done[1].sem, xh_done[1].at(b, (2, 5)[i]))
                rows = lambda name: col(name).unsqueeze(1).to_broadcast([P, T, C])
                pool.tensor_tensor(scaled[:, :, :], xh[1][:, :, :], rows(g), ALU.mult)
                pool.drain()
                pool.tensor_tensor(X1[:, :, :], scaled[:, :, :], rows(beta), ALU.add).then_inc(affine_done[1].sem, 1)

            def scores_b(ph, b, r, a, h):
                if a != 2:
                    return
                pool.wait_ge(exp_done[1].sem, exp_done[1].at(b, h + 1))
                settle(pool)
                view = probs[1][:, h % PR, :].rearrange("p (a n) -> p a n", a=4)[:, 0:4:3, :]
                pool.affine_select(out=masked[:, h % PR, :, :], in_=view, compare_op=ALU.is_gt, fill=0.0, base=0,
                                   pattern=[[0, 2], [-1, P]], channel_multiplier=1).then_inc(masked_done[1].sem, 1)

            def back(ph, b, r, n):
                if ph == 0 or n not in (0, 2):
                    return
                pool.wait_ge(back_done[1].sem, back_done[1].at(b, n + 1))
                if n == 0:
                    pool.tensor_tensor(XS[:, :, :], XO[:, :, :], X1[:, :, :], ALU.add).then_inc(xs_done[1].sem, 1)
                else:
                    pool.tensor_tensor(scaled[:, :, :], XO[:, :, :], X1[:, :, :], ALU.add)
                    pool.drain()
                    pool.tensor_tensor(XS[:, :, :], scaled[:, :, :], X0[:, :, :], ALU.add).then_inc(xs_done[1].sem, 1)

            def reload(ph, b, e):
                pool.wait_ge(y_done[ph].sem, y_done[ph].at(b, e + 1))
                settle(pool)
                pool.dma_start(piece[ph][:, e % PIECES, :], pieces[ph][(e + PIECES) % NEXP[ph]]).then_inc(
                    loaded[ph][e % PIECES].sem, 16)

            def expert(ph, b, r, e):
                if e >= 2:
                    reload(ph, b, e - 2)

            def expert_last(ph, b, r, n):
                reload(ph, b, NEXP[ph] - 2)
                reload(ph, b, NEXP[ph] - 1)

            drive(pool, dict(ln_stats=ln_stats, affine=affine, scores_b=scores_b, back=back, expert=expert, expert_last=expert_last))
            for ph in (0, 1):
                for s in range(PIECES):
                    pool.wait_ge(loaded[ph][s].sem, loaded[ph][s].per * NB + 16)

        @block.tensor
        def _(pe):
            pe.wait_ge(s_const, 2)
            pe.wait_ge(s_ready, 2)
            pe.wait_ge(s_res[0], 16)
            pe.wait_ge(s_res[1], 16)

            def begin(ph, b, r):
                s = r % RING
                pe.wait_ge(free[ph][s].sem, free[ph][s].at(b, r // RING + 1))
                return ring[ph][s]

            def begin_acc(ph, b, n):
                pe.wait_ge(acc_free[ph].sem, acc_free[ph].at(b, n + 1))
                return acc[ph]

            def end(ph, r, ins):
                ins.then_inc(full[ph][r % RING].sem, 1)

            def turn_tile(ph, b, r, tile, width):
                bank = begin(ph, b, r)
                settle(pe)
                for t in range(T):
                    ins = pe.transpose(bank[0:width, t * P:(t + 1) * P], tile[:, t, 0:width], ident[:, :])
                end(ph, r, ins)

            def turn(ph, b, r, n):
                which = {(0, 0): 1, (0, 2): 2, (1, 1): 4, (1, 2): 6, (1, 4): 8, (1, 5): 9}[ph, n]
                pe.wait_ge(xh_done[ph].sem, xh_done[ph].at(b, which))
                turn_tile(ph, b, r, xh[ph], C)

            def turn_two(ph, b, r, n):
                pe.wait_ge(xh_done[1].sem, xh_done[1].at(b, 3))
                turn_tile(1, b, r, xh[1], C)

            def turn_context(ph, b, r, n):
                if ph == 0:
                    pe.wait_ge(c_loaded[0].sem, c_loaded[0].at(b, 16))
                    turn_tile(0, b, r, ctok[0], CC)
                else:
                    pe.wait_ge(xh_done[1].sem, xh_done[1].at(b, 7))
                    turn_tile(1, b, r, xh[1], CC)

            def sources(a):
                return {0: (xT[0], xT[0]), 1: (xT[0], cT[0]), 2: (xT[1], yT), 3: (xT[1], cT[1])}[a]

            def project(ph, b, r, weight, src, rows):
                for c in range(NC):
                    bank = begin(ph, b, r + c)
                    end(ph, r + c, pe.matmul(bank[0:rows, 0:S], col(weight, c * rows, rows), src[:, :], start=True, stop=True))

            def project_q(ph, b, r, a):
                pe.wait_ge(xT_done[ph].sem, xT_done[ph].at(b, {0: 1, 1: 2, 2: 1, 3: 4}[a]))
                if a == 2:
                    pe.wait_ge(yT_done[1].sem, yT_done[1].at(b, 1))
                project(ph, b, r, f"wq{a}", sources(a)[0], 4 * DH[ph])

            def project_k(ph, b, r, a):
                project(ph, b, r, f"wk{a}", sources(a)[1], 4 * DH[ph])

            def project_v(ph, b, r, a):
                if a == 0:
                    pe.wait_ge(xT_done[0].sem, xT_done[0].at(b, 2))
                for t in range(T):
                    bank = begin(ph, b, r + t)
                    end(ph, r + t, pe.matmul(bank[:, :], sources(a)[1][:, t * P:(t + 1) * P], col(f"wv{a}"), start=True, stop=True))

            def scores_a(ph, b, r, a, h):
                n = ordinal(ph, a) + 1
                if h == 0:
                    pe.wait_ge(q_stacked[ph].sem, q_stacked[ph].at(b, 192 * n))
                    pe.wait_ge(k_stacked[ph].sem, k_stacked[ph].at(b, 192 * n))
                bank = begin(ph, b, r)
                for t in range(T):
                    keys = P if a == 0 and t == 0 else S
                    ins = pe.matmul(bank[:, t * S:t * S + keys], qs[ph][0:KROWS, h, t * P:(t + 1) * P],
                                    ks[ph][0:KROWS, h, 0:keys], start=True, stop=True)
                    if a == 0:
                        ins = pe.matmul(bank[:, t * S + t * P:t * S + (t + 1) * P], identb[:, :], mask_qk[:, :],
                                        start=False, stop=True, skip_group_check=True)
                end(ph, r, ins)

            def max_rows(ph, b, r, a):
                n = ordinal(ph, a) + 1
                pe.wait_ge(max_done[ph].sem, max_done[ph].at(b, 16 * n))
                bank = begin(ph, b, r)
                for t in range(T):
                    ins = pe.transpose(bank[0:H, t * P:(t + 1) * P], negmax[ph][:, t, :], ident[:, :])
                end(ph, r, ins)

            def scores_b(ph, b, r, a, h):
                if h == 0:
                    pe.wait_ge(m_stacked[ph].sem, m_stacked[ph].at(b, 32 * (ordinal(ph, a) + 1)))
                bank = begin(ph, b, r)
                for t in range(T):
                    q0 = t * P if a == 0 else 0
                    ins = pe.matmul(bank[:, t * S + q0:(t + 1) * S], ks[ph][0:MROW + 2, h, t * P:(t + 1) * P],
                                    qs[ph][0:MROW + 2, h, q0:S], start=True, stop=True)
                    if a == 0:
                        ins = pe.matmul(bank[:, t * S + q0:t * S + q0 + P], identb[:, :], mask_kq[:, :],
                                        start=False, stop=True, skip_group_check=True)
                end(ph, r, ins)

            def values(ph, b, r, a, c):
                n = ordinal(ph, a)
                pe.wait_ge(exp_done[ph].sem, exp_done[ph].at(b, 16 * n + 4 * c + 4))
                if c == 0:
                    pe.wait_ge(v_done[ph].sem, v_done[ph].at(b, 2 * n + 2))
                    begin_acc(ph, b, (0, 1, 0, 2)[a])
                if a == 2:
                    pe.wait_ge(masked_done[1].sem, masked_done[1].at(b, 4 * c + 4))
                bank = begin(ph, b, r)

                def product(j, t, q0, q1, rhs, start, stop):
                    h = 4 * c + j
                    return pe.matmul(bank[HR * j:HR * (j + 1), q0:q1], V[ph][:, t, HR * h:HR * (h + 1)], rhs,
                                     start=start, stop=stop, tile_position=(0, HR * j), skip_group_check=True)

                def prob(j, t, q0, q1):
                    return probs[ph][:, (4 * c + j) % PR, t * S + q0:t * S + q1]

                if a == 2:
                    for j in range(4):
                        product(j, 1, P, S, masked[:, (4 * c + j) % PR, 1, :], True, True)
                    for j in range(4):
                        product(j, 0, 0, P, masked[:, (4 * c + j) % PR, 0, :], True, False)
                    for j in range(4):
                        ins = product(j, 1, 0, P, prob(j, 1, 0, P), False, True)
                else:
                    for t in range(T):
                        q0 = t * P if a == 0 else 0
                        for j in range(4):
                            ins = product(j, t, q0, S, prob(j, t, q0, S), t == 0, t == T - 1)
                end(ph, r, ins)
                for t in range(T):
                    q0 = t * P if a == 0 else 0
                    for j in range(4):
                        ins = pe.matmul(acc[ph][HR * j:HR * (j + 1), q0:S], sum_lhs[:, c, :], prob(j, t, q0, S),
                                        start=c == 0 and t == 0, stop=c == NC - 1 and t == T - 1,
                                        tile_position=(0, HR * j), skip_group_check=True)
                if c == NC - 1:
                    ins.then_inc(acc_full[ph].sem, 1)

            def normalize(ph, b, r, a):
                pe.wait_ge(r_done[ph].sem, r_done[ph].at(b, ordinal(ph, a) + 1))
                for c in range(NC):
                    bank = begin(ph, b, r + c)
                    lhs = spread[:, c, :, :].rearrange("p j d -> p (j d)")
                    end(ph, r + c, pe.matmul(bank[:, 0:S], lhs, R[ph][:, :], start=True, stop=True))

            def out_project(ph, b, r, a, n):
                src, weight = {0: (Y0, "wp"), 2: (O[1], "li1_2"), 3: (O[1], "li1_3")}[a]
                pe.wait_ge(on_done[ph].sem, on_done[ph].at(b, 4 if a == 2 else 8))
                bank = begin(ph, b, r)
                for c in range(NC):
                    ins = pe.matmul(bank[:, 0:S], col(weight, c * C, C), src[:, c, :], start=c == 0, stop=c == NC - 1)
                end(ph, r, ins)

            def back(ph, b, r, n):
                pe.wait_ge(f_done[ph].sem, f_done[ph].at(b, n + 1))
                bank = begin(ph, b, r)
                for t in range(T):
                    ins = pe.transpose(bank[:, t * C:(t + 1) * C], F[ph][:, t * P:(t + 1) * P], ident[:, :])
                end(ph, r, ins)

            def mlp(ph, b, r, m, n):
                pe.wait_ge(xT_done[1].sem, xT_done[1].at(b, (2, 5)[m]))
                project(1, b, r, f"li2_{m + 2}", xT[1], P)

            def mlp_out(ph, b, r, m, n):
                bank = begin_acc(1, b, (1, 3)[m])
                for c in range(NC):
                    pe.wait_ge(hidden_done[1].sem, hidden_done[1].at(b, 4 * m + c + 1))
                    ins = pe.matmul(bank[:, 0:S], col(f"li3_{m + 2}", c * C, C), hidden[:, c, :], start=c == 0, stop=c == NC - 1)
                ins.then_inc(acc_full[1].sem, 1)

            def router(ph, b, r):
                pe.wait_ge(xT_done[ph].sem, xT_done[ph].at(b, (3, 6)[ph]))
                bank = begin(ph, b, r)
                ne = NEXPERTS[ph]
                for t in range(T):
                    ins = pe.matmul(bank[:, t * ne:(t + 1) * ne], xT[ph][:, t * P:(t + 1) * P], col(f"rw{ph}"), start=True, stop=True)
                end(ph, r, ins)

            def turn_weights(ph, b, r):
                pe.wait_ge(cw_done[ph].sem, cw_done[ph].at(b, 1))
                turn_tile(ph, b, r, cw[ph], NEXPERTS[ph])

            def expert_sum(ph, b, e):
                if e < NROUTED[ph]:
                    pe.wait_ge(gated[ph].sem, gated[ph].at(b, e + 1))
                else:
                    pe.wait_ge(act_done[ph].sem, act_done[ph].at(b, e + 1))
                last = e == NEXP[ph] - 1
                ins = pe.matmul(acc[ph][:, 0:S], piece[ph][:, e % PIECES, C:2 * C], G[ph][:, e % 2, :], start=False, stop=last)
                ins.then_inc(y_done[ph].sem, 1)
                return ins

            def expert(ph, b, r, e):
                s = e % PIECES
                if e == 0:
                    pe.wait_ge(cs_hi[ph].sem, cs_hi[ph].at(b, 1))
                    pe.wait_ge(cs_lo[ph].sem, cs_lo[ph].at(b, 1))
                    bank = begin_acc(ph, b, (2, 4)[ph])
                    pe.matmul(bank[:, 0:S], b2hi[ph][:, :], CS[ph][:, :], start=True, stop=False)
                    pe.matmul(bank[:, 0:S], b2lo[ph][:, :], CS[ph][:, :], start=False, stop=False)
                pe.wait_ge(loaded[ph][s].sem, loaded[ph][s].at(b, 16 * (e // PIECES + 1)))
                bank = begin(ph, b, r)
                end(ph, r, pe.matmul(bank[:, 0:S], piece[ph][:, s, 0:C], xT[ph][:, :], start=True, stop=True))
                if e < NROUTED[ph]:
                    bank = begin(ph, b, r + 1)
                    if ph == 0:
                        lhs = pick0[:, e:e + 1].to_broadcast([P, P])
                    else:
                        lhs = pick1[:, 4 * e:4 * e + 4, :].rearrange("p e d -> p (e d)")
                    end(ph, r + 1, pe.matmul(bank[:, 0:S], lhs, CS[ph][:, :], start=True, stop=True))
                if e >= 1:
                    expert_sum(ph, b, e - 1)

            def expert_last(ph, b, r, n):
                expert_sum(ph, b, NEXP[ph] - 1)
                pe.wait_ge(y_done[ph].sem, y_done[ph].at(b, NEXP[ph]))
                pe.sem_inc(acc_full[ph].sem, 1)

            drive(pe, dict(turn=turn, turn_two=turn_two, turn_context=turn_context, project_q=project_q, project_k=project_k,
                           project_v=project_v, scores_a=scores_a, max_rows=max_rows, scores_b=scores_b, values=values,
                           normalize=normalize, out_project=out_project, back=back, mlp=mlp, mlp_out=mlp_out, router=router,
                           turn_weights=turn_weights, expert=expert, expert_last=expert_last))

        @block.scalar
        def _(act):
            act.wait_ge(s_res[0], 16)
            act.wait_ge(s_res[1], 16)
            for ph in (0, 1):
                b2 = col(("eb2", "fb2")[ph])
                act.activation(b2hi[ph][:, :], b2, ACT.Copy).then_inc(s_ones, 1)
            act.wait_ge(s_const, 2)
            act.wait_ge(s_ready, 2)

            def read(ph, b, r):
                s = r % RING
                act.wait_ge(full[ph][s].sem, full[ph][s].at(b, r // RING + 1))
                return ring[ph][s]

            def release(ph, r, ins):
                ins.then_inc(free[ph][r % RING].sem, 1)

            def turn(ph, b, r, n):
                bank = read(ph, b, r)
                aff = {(1, 1): ("g3_2", "b3_2"), (1, 2): ("gx_3", "bx_3"), (1, 4): ("g3_3", "b3_3")}.get((ph, n))
                if aff:
                    ins = act.activation(xT[ph][:, :], bank[:, 0:S], ACT.Identity, bias=col(aff[1]), scale=col(aff[0]))
                else:
                    ins = act.activation(xT[ph][:, :], bank[:, 0:S], ACT.Copy)
                release(ph, r, ins)
                act.drain()
                act.sem_inc(xT_done[ph].sem, 1)

            def turn_two(ph, b, r, n):
                bank = read(1, b, r)
                act.activation(xT[1][:, :], bank[:, 0:S], ACT.Identity, bias=col("bx_2"), scale=col("gx_2")).then_inc(xT_done[1].sem, 1)

            def turn_context(ph, b, r, n):
                bank = read(ph, b, r)
                if ph == 0:
                    ins = act.activation(cT[0][0:CC, :], bank[0:CC, 0:S], ACT.Copy)
                else:
                    ins = act.activation(cT[1][0:CC, :], bank[0:CC, 0:S], ACT.Identity, bias=col("by_3")[0:CC], scale=col("gy_3")[0:CC])
                release(ph, r, ins)
                act.drain()
                act.sem_inc(xT_done[ph].sem, 1)

            def high_parts(ph, b, r, a, bias):
                n = 4 * DH[ph]
                for c in range(NC):
                    bank = read(ph, b, r + c)
                    if bias:
                        ins = act.activation(SH[ph][0:n, c, :], bank[0:n, 0:S], ACT.Identity, bias=col(bias, c, 1)[0:n])
                    else:
                        ins = act.activation(SH[ph][0:n, c, :], bank[0:n, 0:S], ACT.Copy)
                    ins.then_inc(hi_done[ph].sem, 1)

            def project_q(ph, b, r, a):
                high_parts(ph, b, r, a, f"bq{a}" if ph == 0 else None)

            def project_k(ph, b, r, a):
                act.wait_ge(q_stacked[ph].sem, q_stacked[ph].at(b, 192 * (ordinal(ph, a) + 1)))
                high_parts(ph, b, r, a, f"bk{a}" if ph == 0 else None)

            def project_v(ph, b, r, a):
                for t in range(T):
                    bank = read(ph, b, r + t)
                    ins = act.activation(V[ph][:, t, :], bank[:, :], ACT.Copy)
                    release(ph, r + t, ins)
                act.drain()
                act.sem_inc(v_done[ph].sem, 2)

            def max_rows(ph, b, r, a):
                bank = read(ph, b, r)
                act.activation(MH[ph][:, :], bank[0:H, 0:S], ACT.Copy).then_inc(mh_done[ph].sem, 1)

            def scores_b(ph, b, r, a, h):
                bank = read(ph, b, r)
                scale = float(DH[ph]) ** -0.5
                if a == 0:
                    act.activation(probs[ph][:, h % PR, 0:S], bank[:, 0:S], ACT.Exp, scale=scale)
                    ins = act.activation(probs[ph][:, h % PR, S + P:2 * S], bank[:, S + P:2 * S], ACT.Exp, scale=scale)
                else:
                    ins = act.activation(probs[ph][:, h % PR, :], bank[:, :], ACT.Exp, scale=scale)
                release(ph, r, ins)
                act.drain()
                act.sem_inc(exp_done[ph].sem, 1)

            def values(ph, b, r, a, c):
                bank = read(ph, b, r)
                ins = act.activation(O[ph][:, c, :], bank[:, 0:S], ACT.Copy)
                release(ph, r, ins)
                act.drain()
                act.sem_inc(o_done[ph].sem, 1)

            def feature_result(ph, src, bias):
                return act.activation(F[ph][:, :], src, ACT.Identity, bias=bias)

            def out_project(ph, b, r, a, n):
                bank = read(ph, b, r)
                ins = feature_result(ph, bank[:, 0:S], col({0: "bp", 2: "li1b_2", 3: "li1b_3"}[a]))
                release(ph, r, ins)
                act.drain()
                act.sem_inc(f_done[ph].sem, 1)

            def acc_result(ph, b, n, bias):
                act.wait_ge(acc_full[ph].sem, acc_full[ph].at(b, n + 1))
                feature_result(ph, acc[ph][:, 0:S], bias).then_inc(acc_free[ph].sem, 1)
                act.drain()
                act.sem_inc(f_done[ph].sem, 1)

            def mlp(ph, b, r, m, n):
                for c in range(NC):
                    bank = read(1, b, r + c)
                    ins = act.activation(hidden[:, c, :], bank[:, 0:S], ACT.Gelu, bias=col(f"li2b_{m + 2}", c, 1))
                    release(1, r + c, ins)
                    act.drain()
                    act.sem_inc(hidden_done[1].sem, 1)

            def mlp_out(ph, b, r, m, n):
                acc_result(1, b, (1, 3)[m], col(f"li3b_{m + 2}"))

            def router(ph, b, r):
                act.wait_ge(logits_done[ph].sem, logits_done[ph].at(b, 1))
                for t in range(T):
                    ins = act.activation(expl[ph][:, t, :], logits[ph][:, t, 0:NEXPERTS[ph]], ACT.Exp, bias=nmx[ph][:, t:t + 1],
                                         accum_out=esum[ph][:, t:t + 1])
                ins.then_inc(expl_done[ph].sem, 1)

            def turn_weights(ph, b, r):
                bank = read(ph, b, r)
                ne = NEXPERTS[ph]
                act.activation(CS[ph][0:ne, :], bank[0:ne, 0:S], ACT.Copy).then_inc(cs_hi[ph].sem, 1)

            def expert(ph, b, r, e):
                bank = read(ph, b, r)
                f, bias = (ACT.Relu, "eb1") if ph == 0 else (ACT.Silu, "fb1")
                dst = Hx if e < NROUTED[ph] else G
                ins = act.activation(dst[ph][:, e % 2, :], bank[:, 0:S], f, bias=col(bias, e, 1))
                release(ph, r, ins)
                act.drain()
                act.sem_inc(act_done[ph].sem, 1)

            def expert_last(ph, b, r, n):
                acc_result(ph, b, (2, 4)[ph], col("sb2") if ph == 0 else fsb2_sum[:, :])

            drive(act, dict(turn=turn, turn_two=turn_two, turn_context=turn_context, project_q=project_q, project_k=project_k,
                            project_v=project_v, max_rows=max_rows, scores_b=scores_b, values=values, out_project=out_project,
                            mlp=mlp, mlp_out=mlp_out, router=router, turn_weights=turn_weights, expert=expert,
                            expert_last=expert_last))

        @block.vector
        def _(dve):
            dve.memset(sum_lhs[:, :, :], 1.0)
            dve.drain()
            dve.memset(sum_lhs[:, :, 0:NC], 0.0)
            dve.memset(logits[0][:, :, :], SENT)
            dve.memset(take3[:, :, :], SENT)
            dve.drain()
            for c in range(NC):
                dve.memset(sum_lhs[:, c, c:c + 1], 1.0)
            for ph in (0, 1):
                for s in range(RING):
                    dve.memset(ring[ph][s][:, :], 0.0).then_inc(free[ph][s].sem, 1)
                dve.memset(acc[ph][:, :], 1.0).then_inc(acc_free[ph].sem, 1)
            dve.wait_ge(s_const, 1)
            dve.tensor_tensor(pick0[:, :], ident[:, 0:E0], ident[:, 32:32 + E0], ALU.add)
            wide = lambda at: ident[:, at:at + E1].unsqueeze(2).to_broadcast([P, E1, HR])
            dve.tensor_tensor(pick1[:, :, :], wide(0), wide(E1), ALU.add)
            for c in range(NC):
                dve.tensor_copy(spread[:, c, :, :], ident[:, c:P:HR].unsqueeze(2).to_broadcast([P, 4, HR]))
            dve.wait_ge(s_res[0], 16)
            dve.wait_ge(s_res[1], 16)
            dve.tensor_tensor(bv_sum[:, :], col("bv0"), col("bv1"), ALU.add)
            dve.tensor_tensor(fsb2_sum[:, :], col("fsb2", 0, 1), col("fsb2", 1, 1), ALU.add)
            dve.wait_ge(s_ones, 2)
            for ph in (0, 1):
                b2 = col(("eb2", "fb2")[ph])
                dve.tensor_tensor(b2lo[ph][:, :], b2, b2hi[ph][:, :].bitcast(F32), ALU.subtract)
            dve.drain()
            dve.sem_inc(s_ready, 2)
            dve.wait_ge(s_const, 2)

            def read(ph, b, r):
                s = r % RING
                dve.wait_ge(full[ph][s].sem, full[ph][s].at(b, r // RING + 1))
                return ring[ph][s]

            def release(ph, r, ins):
                ins.then_inc(free[ph][r % RING].sem, 1)

            def ln_source(ph, i):
                return {(0, 0): xin, (0, 1): x1, (1, 0): X0, (1, 1): xh[1], (1, 2): X1, (1, 3): XO, (1, 4): XS,
                        (1, 5): X1, (1, 6): ctok[1], (1, 7): XO, (1, 8): XS}[ph, i]

            def ln_width(ph, i):
                return CC if (ph, i) == (1, 6) else C

            def ln_stats(ph, b, r, i):
                dve.drain()
                if (ph, i) == (0, 0):
                    dve.wait_ge(x_loaded[0].sem, x_loaded[0].at(b, 16))
                if (ph, i) in ((1, 2), (1, 5)):
                    dve.wait_ge(affine_done[1].sem, affine_done[1].at(b, (i + 1) // 3))
                if (ph, i) == (1, 6):
                    dve.wait_ge(c_loaded[1].sem, c_loaded[1].at(b, 16))
                src, w = ln_source(ph, i), ln_width(ph, i)
                for t in range(T):
                    dve.bn_stats(stats[ph][:, t, :], src[:, t, 0:w])
                dve.drain()
                for t in range(T):
                    dve.bn_aggr(mv[ph][:, t, :], stats[ph][:, t, :])
                dve.drain()
                dve.tensor_scalar(ve[ph][:, :], mv[ph][:, :, 1], EPS, None, ALU.add).then_inc(var_done[ph].sem, 1)

            def ln_apply(ph, b, r, i):
                src, w = ln_source(ph, i), ln_width(ph, i)
                dve.wait_ge(rstd_done[ph].sem, rstd_done[ph].at(b, i + 1))
                if (ph, i) == (1, 6):
                    dve.wait_ge(xT_done[1].sem, xT_done[1].at(b, 3))
                for t in range(T):
                    ins = dve.tensor_scalar(xh[ph][:, t, 0:w], src[:, t, 0:w], mv[ph][:, t, 0:1], rstd[ph][:, t:t + 1],
                                            ALU.subtract, ALU.mult)
                ins.then_inc(xh_done[ph].sem, 1)

            def take(ph, b, r):
                dve.drain()
                dve.tensor_copy(X0[:, :, :], handed[:, :, :])

            def turn_two(ph, b, r, n):
                bank = read(1, b, r)
                dve.wait_ge(xT_done[1].sem, xT_done[1].at(b, 1))
                ins = dve.tensor_scalar(yT[:, :], bank[:, 0:S], col("gy_2"), col("by_2"), ALU.mult, ALU.add)
                release(1, r, ins)
                dve.drain()
                dve.sem_inc(yT_done[1].sem, 1)

            def low_parts(ph, b, r, a, k, bias):
                n = 4 * DH[ph]
                for c in range(NC):
                    read(ph, b, r + c)
                    bank = ring[ph][(r + c) % RING]
                    dve.wait_ge(hi_done[ph].sem, hi_done[ph].at(b, 8 * ordinal(ph, a) + 4 * k + c + 1))
                    high = SH[ph][0:n, c, :].bitcast(F32)
                    if bias:
                        ins = dve.scalar_tensor_tensor(SL[ph][0:n, c, :], bank[0:n, 0:S], col(bias, c, 1)[0:n], high, ALU.add, ALU.subtract)
                    else:
                        ins = dve.tensor_tensor(SL[ph][0:n, c, :], bank[0:n, 0:S], high, ALU.subtract)
                    release(ph, r + c, ins)
                dve.drain()
                dve.sem_inc(lo_done[ph].sem, 4)

            def project_q(ph, b, r, a):
                low_parts(ph, b, r, a, 0, f"bq{a}" if ph == 0 else None)

            def project_k(ph, b, r, a):
                low_parts(ph, b, r, a, 1, f"bk{a}" if ph == 0 else None)

            def scores_a(ph, b, r, a, h):
                bank = read(ph, b, r)
                if a == 0:
                    dve.tensor_reduce(negmax[ph][:, 0, h:h + 1], bank[:, 0:P], AX.X, ALU.max, negate=True)
                    ins = dve.tensor_reduce(negmax[ph][:, 1, h:h + 1], bank[:, S:2 * S], AX.X, ALU.max, negate=True)
                else:
                    ins = dve.tensor_reduce(negmax[ph][:, :, h], bank[:, :].rearrange("p (t n) -> p t n", t=T), AX.X, ALU.max, negate=True)
                release(ph, r, ins)
                if h == H - 1:
                    dve.drain()
                    dve.sem_inc(max_done[ph].sem, 16)

            def max_rows(ph, b, r, a):
                bank = read(ph, b, r)
                dve.wait_ge(mh_done[ph].sem, mh_done[ph].at(b, ordinal(ph, a) + 1))
                ins = dve.tensor_tensor(ML[ph][:, :], bank[0:H, 0:S], MH[ph][:, :].bitcast(F32), ALU.subtract)
                release(ph, r, ins)
                dve.drain()
                dve.sem_inc(ml_done[ph].sem, 1)

            def sums(ph, b, r, a):
                dve.wait_ge(acc_full[ph].sem, acc_full[ph].at(b, (1, 2, 1, 3)[a]))
                dve.reciprocal(R[ph][:, :], acc[ph][:, 0:S]).then_inc(acc_free[ph].sem, 1)
                dve.drain()
                dve.sem_inc(r_done[ph].sem, 1)

            def normalize(ph, b, r, a):
                n = ordinal(ph, a)
                dve.wait_ge(o_done[ph].sem, o_done[ph].at(b, 4 * n + 4))
                for c in range(NC):
                    bank = read(ph, b, r + c)
                    dst = Y0 if a == 0 else O[ph]
                    ins = dve.tensor_tensor(dst[:, c, :], bank[:, 0:S], O[ph][:, c, :], ALU.mult)
                    release(ph, r + c, ins)
                dve.drain()
                if a == 1:
                    for c in range(NC):
                        dve.scalar_tensor_tensor(Y0[:, c, :], O[0][:, c, :], bv_sum[:, c:c + 1], Y0[:, c, :], ALU.add, ALU.add)
                    dve.drain()
                dve.sem_inc(on_done[ph].sem, 4)

            def back(ph, b, r, n):
                bank = read(ph, b, r)
                dst, other = {(0, 0): (x1, xin), (0, 1): (handed, x1), (1, 0): (XO, X1), (1, 1): (XS, XS), (1, 2): (XO, X1),
                              (1, 3): (XS, XS), (1, 4): (result, XS)}[ph, n]
                if (ph, n) in ((1, 1), (1, 3)):
                    dve.wait_ge(xs_done[1].sem, xs_done[1].at(b, (n + 1) // 2))
                flat = lambda tile: tile[:, :, :].rearrange("p t c -> p (t c)")
                ins = dve.tensor_tensor(flat(dst), bank[:, 0:T * C], flat(other), ALU.add)
                release(ph, r, ins)
                dve.drain()
                dve.sem_inc(back_done[ph].sem, 1)

            def router(ph, b, r):
                bank = read(ph, b, r)
                ne = NEXPERTS[ph]
                rb = col(f"rb{ph}").unsqueeze(1).to_broadcast([P, T, ne])
                ins = dve.tensor_tensor(logits[ph][:, :, 0:ne], bank[:, 0:T * ne].rearrange("p (t e) -> p t e", t=T), rb, ALU.add)
                release(ph, r, ins)
                dve.drain()
                for t in range(T):
                    dve.max(top8[ph][:, t, :], logits[ph][:, t, :])
                dve.drain()
                dve.tensor_scalar(nmx[ph][:, :], top8[ph][:, :, 0], -1.0, None, ALU.mult).then_inc(logits_done[ph].sem, 1)
                found = top8[1]
                if ph == 0:
                    dve.tensor_copy(take3[:, :, 0:K0], top8[0][:, :, 0:K0])
                    dve.drain()
                    found = take3
                for t in range(T):
                    dve.match_replace(left[ph][:, t, :], found[:, t, :], logits[ph][:, t, :], TAKEN)
                dve.drain()
                dve.tensor_tensor(chosen[ph][:, :, :], left[ph][:, :, 0:ne], logits[ph][:, :, 0:ne], ALU.not_equal)
                dve.drain()
                dve.wait_ge(expl_done[ph].sem, expl_done[ph].at(b, 1))
                if ph == 1:
                    dve.tensor_tensor(expl[1][:, :, :], expl[1][:, :, :], chosen[1][:, :, :], ALU.mult)
                    dve.drain()
                    dve.tensor_reduce(esum[1][:, :], expl[1][:, :, :], AX.X, ALU.add)
                    dve.drain()
                dve.reciprocal(esum[ph][:, :], esum[ph][:, :])
                dve.drain()
                for t in range(T):
                    ins = dve.scalar_tensor_tensor(cw[ph][:, t, :], expl[ph][:, t, :], esum[ph][:, t:t + 1], chosen[ph][:, t, :],
                                                   ALU.mult, ALU.mult)
                ins.then_inc(cw_done[ph].sem, 1)

            def turn_weights(ph, b, r):
                bank = read(ph, b, r)
                ne, at = NEXPERTS[ph], (32, 64)[ph]
                dve.wait_ge(cs_hi[ph].sem, cs_hi[ph].at(b, 1))
                ins = dve.tensor_tensor(CS[ph][at:at + ne, :], bank[0:ne, 0:S], CS[ph][0:ne, :].bitcast(F32), ALU.subtract)
                release(ph, r, ins)
                dve.drain()
                dve.sem_inc(cs_lo[ph].sem, 1)

            def expert(ph, b, r, e):
                if e >= NROUTED[ph]:
                    return
                bank = read(ph, b, r + 1)
                dve.wait_ge(act_done[ph].sem, act_done[ph].at(b, e + 1))
                ins = dve.tensor_tensor(G[ph][:, e % 2, :], bank[:, 0:S], Hx[ph][:, e % 2, :], ALU.mult)
                release(ph, r + 1, ins)
                dve.drain()
                dve.sem_inc(gated[ph].sem, 1)

            drive(dve, dict(ln_stats=ln_stats, ln_apply=ln_apply, take=take, turn_two=turn_two, project_q=project_q,
                            project_k=project_k, scores_a=scores_a, max_rows=max_rows, sums=sums, normalize=normalize, back=back,
                            router=router, turn_weights=turn_weights, expert=expert))


def _pad_rows(a):
    return np.concatenate([a, np.zeros((P - a.shape[0],) + a.shape[1:], a.dtype)]) if a.shape[0] < P else a


def _head_columns(w):
    c = w.shape[0]
    out = np.zeros((c, H, HR), w.dtype)
    out[:, :, :D0] = w.reshape(c, H, D0)
    return _pad_rows(out.reshape(c, H * HR))


def _head_vector(v):
    out = np.zeros((NC, 4, HR), v.dtype)
    out[:, :, :D0] = v.reshape(NC, 4, D0)
    return out.reshape(NC, P).T


def _chunk_rows(w):
    return w.reshape(-1, P, w.shape[1]).transpose(1, 0, 2).reshape(P, -1)


def _row_everywhere(v):
    return np.broadcast_to(v[None, :], (P, v.shape[0]))


def lay_out(a):
    L0 = lambda n: a["L0_xattn_" + n]
    L1 = lambda n: a["L1_xattn_" + n]
    cols = {"L1": np.zeros((P, 0), np.float32)}
    for i, p in ((0, ""), (1, "c")):
        for n in "qk":
            cols[f"w{n}{i}"] = _pad_rows(L0(f"W{p}{n}"))
            cols[f"b{n}{i}"] = _pad_rows(L0(f"b{p}{n}").reshape(NC, 4 * D0).T)
        cols[f"wv{i}"] = _head_columns(L0(f"W{p}v"))
        cols[f"bv{i}"] = _head_vector(L0(f"b{p}v"))
    wp = np.zeros((NC, 4, HR, C), np.float32)
    wp[:, :, :D0, :] = L0("Wp").reshape(NC, 4, D0, C)
    cols["wp"] = _chunk_rows(wp.reshape(NC * P, C))
    cols["bp"] = L0("bp")[:, None]
    cols["rw0"] = a["L0_ffn_router_W"]
    cols["rb0"] = _row_everywhere(a["L0_ffn_router_b"])
    cols["eb1"] = np.concatenate([a["L0_ffn_eb1"], a["L0_ffn_sb1"][None]]).T
    eb2 = np.zeros((P, C), np.float32)
    eb2[0:E0] = a["L0_ffn_eb2"]
    eb2[32:32 + E0] = a["L0_ffn_eb2"]
    cols["eb2"] = eb2
    cols["sb2"] = a["L0_ffn_sb2"][:, None]
    for i, p in ((2, "a1_"), (3, "a2_")):
        for n in "qkv":
            w = L1(p + "w" + n)
            cols[f"w{n}{i}"] = _pad_rows(w.transpose(1, 0, 2).reshape(w.shape[1], H * D1))
        cols[f"li1_{i}"] = _chunk_rows(L1(p + "li1_w"))
        cols[f"li2_{i}"] = L1(p + "li2_w")
        cols[f"li3_{i}"] = _chunk_rows(L1(p + "li3_w"))
        cols[f"li1b_{i}"] = L1(p + "li1_b")[:, None]
        cols[f"li2b_{i}"] = L1(p + "li2_b").reshape(NC, P).T
        cols[f"li3b_{i}"] = L1(p + "li3_b")[:, None]
        for g, n in (("x", "lnx"), ("y", "lny"), ("3", "ln3")):
            cols[f"g{g}_{i}"] = _pad_rows(L1(p + n + "_g")[:, None])
            cols[f"b{g}_{i}"] = _pad_rows(L1(p + n + "_b")[:, None])
    for n in ("ln1", "ln2"):
        cols[n + "g"] = _row_everywhere(L1(n + "_g"))
        cols[n + "b"] = _row_everywhere(L1(n + "_b"))
    cols["rw1"] = a["L1_ffn_router_w"]
    cols["rb1"] = _row_everywhere(a["L1_ffn_router_b"])
    cols["fb1"] = np.concatenate([a["L1_ffn_b1"].reshape(NR1, P), a["L1_ffn_sb1"].reshape(-1, P)]).T
    cols["fb2"] = np.concatenate([a["L1_ffn_b2"], a["L1_ffn_b2"]])
    cols["fsb2"] = a["L1_ffn_sb2"].T
    resident = np.concatenate([cols[n] for n in COLS], axis=1)
    assert resident.shape == (P, NCOLS)
    w1 = np.concatenate([a["L0_ffn_eW1"], a["L0_ffn_sW1"][None]])
    w2 = np.concatenate([a["L0_ffn_eW2"], a["L0_ffn_sW2"][None]])
    pieces0 = np.concatenate([w1, w2], axis=2)
    w1 = np.concatenate([a["L1_ffn_w1"].reshape(NR1, 4, C, 32).transpose(0, 2, 1, 3).reshape(NR1, C, P),
                         a["L1_ffn_sw1"].reshape(2, C, 2, P).transpose(0, 2, 1, 3).reshape(4, C, P)])
    w2 = np.concatenate([a["L1_ffn_w2"].reshape(NR1, P, C), a["L1_ffn_sw2"].reshape(4, P, C)])
    pieces1 = np.concatenate([w1, w2], axis=2)
    return {"in_resident": resident, "in_pieces0": pieces0, "in_pieces1": pieces1,
            "in_x": a["x"], "in_ctx": a["ctx_512"]}


def kernel(**inputs):
    import concourse.bacc as bacc
    from concourse.bass_utils import run_bass_kernel_spmd

    arrays = {n: np.ascontiguousarray(v) for n, v in lay_out({n: np.asarray(v) for n, v in inputs.items()}).items()}
    nc = bacc.Bacc("TRN2", target_bir_lowering=False, num_devices=1)
    args = [nc.dram_tensor(n, v.shape, mybir.dt.from_np(v.dtype), kind="ExternalInput").ap() for n, v in arrays.items()]
    out = nc.dram_tensor("out", (NB, S, C), F32, kind="ExternalOutput").ap()
    build(nc, *args, out)
    r = run_bass_kernel_spmd(nc, [arrays], core_ids=[0])
    return r.results[0]["out"]
```

```python
from contextlib import ExitStack

import numpy as np

import concourse.bass as bass
from concourse import mybir

F32 = mybir.dt.float32
F32R = mybir.dt.float32r
BF16 = mybir.dt.bfloat16
ALU = mybir.AluOpType
ACT = mybir.ActivationFunctionType
AX = mybir.AxisListType

P = 128
NB = 8
S = 256
T = S // P
C = 128
CC = 64
H = 16
HR = 32
NC = H * HR // P
D0, D1 = 8, 32
E0, K0 = 15, 3
E1, K1 = 64, 8
NE0 = E0 + 1
NR1 = E1 * 32 // P
NE1 = NR1 + 2 * 256 // P
EPS = 1e-5
NEG = -1e30
SENT = -2e30
TAKEN = -3e30
RING = 3
PR = 5
SLOTS = 4
LAG = 2
KROWS = 3 * HR
MROW = KROWS
LPAD = 20


def columns():
    at, out = 0, {}
    for name, n in [
        ("wqkq", NC * 96), ("wk1", NC * 32), ("bqkqk", NC), ("wv0", C), ("wv1", C), ("bv0", NC), ("bv1", NC),
        ("wp", 512), ("bp", 1), ("rw0", E0), ("rb0", E0), ("eb1", NE0), ("eb2", C), ("sb2", 1),
        ("L1", 0),
        ("wq2", 512), ("wk2", 512), ("wv2", 512), ("li1_2", 512), ("li2_2", 512), ("li3_2", 512),
        ("wq3", 512), ("wk3", 512), ("wv3", 512), ("li1_3", 512), ("li2_3", 512), ("li3_3", 512),
        ("li1b_2", 1), ("li2b_2", 4), ("li3b_2", 1), ("li1b_3", 1), ("li2b_3", 4), ("li3b_3", 1),
        ("gx_2", 1), ("bx_2", 1), ("gy_2", 1), ("by_2", 1), ("g3_2", 1), ("b3_2", 1),
        ("gx_3", 1), ("bx_3", 1), ("gy_3", 1), ("by_3", 1), ("g3_3", 1), ("b3_3", 1),
        ("ln1g", C), ("ln1b", C), ("ln2g", C), ("ln2b", C),
        ("rw1", E1), ("rb1", E1), ("fb1", NE1), ("fb2", C), ("fsb2", 2),
    ]:
        out[name] = (at, n)
        at += n
    return out, at


COLS, NCOLS = columns()


def phase_steps(ph):
    def attention(a):
        for h in range(H):
            yield "scores_a", (a, h), 1
        yield "max_rows", (a,), 1
        for h in range(H):
            yield "scores_b", (a, h), 1
            if h >= PR - 1 and (h - PR + 1) % 4 == 0:
                yield "values", (a, (h - PR + 1) // 4), 1
            if h == 6 and a == 2:
                yield from norm(2)
            if h == 10 and a == 2:
                yield "turn_context", (3,), 1
                yield "project_k", (3,), 4
        if a in (0, 2):
            if a == 0:
                yield "stack_q", (1,), 0
            yield "stack_k", (a + 1,), 0
        yield "values", (a, NC - 1), 1
        if a in (1, 3):
            yield "load_experts", (a,), 0
        yield "sums", (a,), 0
        yield "normalize", (a,), NC

    def back(n):
        yield "back", (n,), 1

    def norm(i):
        yield "ln_stats", (i,), 0
        yield "ln_apply", (i,), 0

    if ph == 0:
        yield "load", (), 0
        yield from norm(0)
        yield "turn_context", (1,), 1
        yield "turn", (0,), 1
        yield "project_all", (), NC
        yield "stack_q", (0,), 0
        yield "stack_k", (0,), 0
        yield "project_values", (), T
        yield "wait", (0,), 0
        yield from attention(0)
        yield from attention(1)
        yield "out_project", (0, 0), 1
        yield from back(0)
        yield from norm(1)
        yield "turn", (2,), 1
        yield "router", (), 1
        yield "turn_weights", (), 1
        for e in range(NE0):
            yield "expert", (e,), 1
        yield "expert_last", (1,), 0
        yield from back(1)
        yield "even_out", (), 2
    else:
        yield "load", (), 0
        yield from norm(0)
        yield "take", (), 0
        yield "affine", (0,), 0
        yield from norm(1)
        yield "turn_two", (0,), 1
        yield "project_q", (2,), 4
        yield "stack_q", (2,), 0
        yield "project_k", (2,), 4
        yield "stack_k", (2,), 0
        yield "project_v", (2,), 2
        yield "wait", (2,), 0
        yield from attention(2)
        yield "out_project", (2, 0), 1
        yield from back(0)
        yield from norm(3)
        yield "turn", (1,), 1
        yield "mlp", (0, 1), 4
        yield "mlp_out", (0, 1), 0
        yield from back(1)
        yield from norm(4)
        yield "affine", (1,), 0
        yield from norm(5)
        yield "turn", (2,), 1
        yield "project_q", (3,), 4
        yield "stack_q", (3,), 0
        yield "project_v", (3,), 2
        yield "wait", (3,), 0
        yield from attention(3)
        yield "out_project", (3, 2), 1
        yield from back(2)
        yield from norm(6)
        yield "turn", (4,), 1
        yield "mlp", (1, 3), 4
        yield "mlp_out", (1, 3), 0
        yield from back(3)
        yield from norm(7)
        yield "turn", (5,), 1
        yield "router", (), 1
        yield "turn_weights", (), 1
        for e in range(NE1):
            yield "expert", (e,), 1
        yield "expert_last", (4,), 0
        yield from back(4)
        yield "store", (), 0
        yield "even_out", (), 2


def numbered(ph):
    out, r = [], 0
    for name, args, uses in phase_steps(ph):
        out.append((name, ph, r, args))
        r += uses
    return out, r


STEPS = [numbered(ph)[0] for ph in (0, 1)]
USES = [numbered(ph)[1] for ph in (0, 1)]
assert all(n % RING == 0 for n in USES)


HEAD = 7
LENGTHS = [
    {"load": 2, "ln_stats 0": 1.196, "ln_apply 0": 1, "turn_context 1": 0.8, "turn 0": 0.81, "project_all": 2.758,
     "stack_q 0": 2, "stack_k 0": 0, "project_values": 1, "wait 0": 10, "scores_a 0": 0.6, "max_rows 0": 4,
     "scores_b 0": 0.5, "values 0": 2.2, "stack_q 1": 0, "stack_k 1": 2.0, "sums 0": 5.992, "normalize 0": 0.89,
     "scores_a 1": 0.6, "max_rows 1": 2.63, "scores_b 1": 0.5, "values 1": 2.2, "load_experts 1": 0, "sums 1": 1.112,
     "normalize 1": 1.8, "out_project 0": 2.915, "back 0": 1.2, "ln_stats 1": 1.5, "ln_apply 1": 1, "turn 2": 0.8,
     "router": 6, "turn_weights": 2.253, "expert": 0.6, "expert_last 1": 1.5, "back 1": 1.2, "even_out": 0},
    {"load": 0, "ln_stats 0": 1.5, "ln_apply 0": 1.74, "take": 0.365, "affine 0": 2, "ln_stats 1": 1.168,
     "ln_apply 1": 1.78, "turn_two 0": 2.453, "project_q 2": 1.349, "stack_q 2": 0, "project_k 2": 1.8,
     "stack_k 2": 0, "project_v 2": 1.8, "wait 2": 20.893, "scores_a 2": 0.6, "max_rows 2": 4, "scores_b 2": 0.5,
     "values 2": 2.2, "ln_stats 2": 2.739, "ln_apply 2": 1, "turn_context 3": 2.92, "project_k 3": 1.8,
     "stack_k 3": 0, "sums 2": 0.495, "normalize 2": 7.018, "out_project 2": 2.2, "back 0": 1.2, "ln_stats 3": 1.5,
     "ln_apply 3": 1, "turn 1": 1.111, "mlp 0": 2.5, "mlp_out 0": 2.5, "back 1": 1.04, "ln_stats 4": 1.5,
     "ln_apply 4": 1.634, "affine 1": 2.762, "ln_stats 5": 1.5, "ln_apply 5": 1, "turn 2": 1.47,
     "project_q 3": 1.274, "stack_q 3": 0, "project_v 3": 1.8, "wait 3": 10, "scores_a 3": 0.6, "max_rows 3": 4,
     "scores_b 3": 1.13, "values 3": 1.381, "load_experts 3": 0, "sums 3": 2, "normalize 3": 1.8,
     "out_project 3": 2.2, "back 2": 1.2, "ln_stats 6": 1.5, "ln_apply 6": 1, "turn 4": 1, "mlp 1": 1.76,
     "mlp_out 1": 2.5, "back 3": 1.2, "ln_stats 7": 1.694, "ln_apply 7": 1, "turn 5": 1, "router": 8.715,
     "turn_weights": 1.12, "expert": 0.6, "expert_last 4": 1.5, "back 4": 1.2, "store": 0, "even_out": 0},
]


def length(step):
    name, ph, _, args = step
    return LENGTHS[ph][name if not args or name == "expert" else f"{name} {args[0]}"]


def merged_order():
    lists = [STEPS[0][HEAD:] + STEPS[0][:HEAD], STEPS[1]]
    total = [sum(map(length, steps)) for steps in lists]
    at, done, out = [0, 0], [0.0, 0.0], []
    while at[0] < len(lists[0]) or at[1] < len(lists[1]):
        left = [ph for ph in (0, 1) if at[ph] < len(lists[ph])]
        ph = min(left, key=lambda q: done[q] / total[q])
        step = lists[ph][at[ph]]
        out.append(step)
        done[ph] += length(step)
        at[ph] += 1
    return out


BOTH = merged_order()
HEADS = {(name, args) for name, _, _, args in STEPS[0][:HEAD]}
USE_OF = {(ph, name, args): r for steps in STEPS for name, ph, r, args in steps}


class Batch:

    def __init__(self, i, plus):
        self.i, self.plus = i, plus

    def times(self, n, more):
        return self.plus * n + more if self.i is None else self.i * n + (self.plus * n + more)


class Signal:

    def __init__(self, sem, per):
        self.sem, self.per = sem, per

    def at(self, b, j):
        return b.times(self.per, j)


def build(nc, resident, pieces0, pieces1, x_in, ctx_in, out):
    with ExitStack() as ctx:
        def sb(name, shape, dt=F32):
            return ctx.enter_context(nc.sbuf_tensor("t_" + name, shape, dt))

        W = sb("resident", [P, NCOLS])

        def col(name, i=0, n=None):
            at, width = COLS[name]
            return W[:, at + i:at + i + (width - i if n is None else n)]

        ident = sb("ident", [P, P])
        identb = sb("identb", [P, P], BF16)
        zerosb = sb("zerosb", [P, P], BF16)
        mask_qk = sb("mask_qk", [P, P], BF16)
        mask_kq = sb("mask_kq", [P, P], BF16)
        pick0 = sb("pick0", [P, E0], F32R)
        pick1 = sb("pick1", [P, E1, HR], F32R)
        spread = sb("spread", [P, NC, 4, HR])
        sum_lhs = sb("sum_lhs", [P, NC, HR])
        minus_half = sb("minus_half", [P, T])
        bv_sum = sb("bv_sum", [P, NC])
        fsb2_sum = sb("fsb2_sum", [P, 1])
        b2hi = [sb(f"b2hi{ph}", [P, C], F32R) for ph in (0, 1)]
        b2lo = [sb(f"b2lo{ph}", [P, C], F32R) for ph in (0, 1)]

        def two(name, shape, dt=F32):
            return [sb(f"{name}{ph}", shape, dt) for ph in (0, 1)]

        xin = sb("xin", [P, T, C])
        x1 = sb("x1", [P, T, C])
        handed = sb("handed", [P, T, C])
        X0 = sb("X0", [P, T, C])
        X1 = sb("X1", [P, T, C])
        XO = sb("XO", [P, T, C])
        XS = sb("XS", [P, T, C])
        scaled = sb("scaled", [P, T, C])
        result = sb("result", [P, T, C])
        ctok = two("ctok", [P, T, CC])
        xh = two("xh", [P, T, C])
        stats = two("stats", [P, T, 6])
        mv = two("mv", [P, T, 2])
        ve = two("ve", [P, T])
        rstd = two("rstd", [P, T])
        xT = two("xT", [P, S])
        yT = sb("yT", [P, S])
        cT = two("cT", [P, S])
        O = two("O", [P, NC, S])
        low = two("low", [P, NC, S])
        Y0 = sb("Y0", [P, NC, S])
        high0 = Y0[:, :, :].bitcast(F32R)
        khigh1 = sb("khigh1", [P, NC, S], F32R)
        masked = sb("masked", [P, PR, 2, P])
        attended = [O[0], Y0, O[1], O[1]]
        parts = {a: [(high0, low[0][:, :, :].bitcast(F32R), HR * (2 * a + i), D0) for i in (0, 1)] for a in (0, 1)}
        q_parts = (O[1][:, :, :].bitcast(F32R), low[1][:, :, :].bitcast(F32R), 0, D1)
        parts[2] = [q_parts, (khigh1, masked[:, 0:NC, :, :].rearrange("p c a n -> p c (a n)").bitcast(F32R), 0, D1)]
        parts[3] = [q_parts, (khigh1, q_parts[1], 0, D1)]
        qs = two("qs", [P, H, S], F32R)
        ks = two("ks", [P, H, S], F32R)
        V = [sb("V0", [P, T, 2 * C]), sb("V1", [P, T, H * HR])]
        negmax = two("negmax", [P, T, H])
        MH = two("MH", [H, S], F32R)
        ML = two("ML", [H, S], F32R)
        probs = two("probs", [P, PR, 2 * S])
        R = two("R", [P, S])
        F = two("F", [P, S])
        hidden = low[1]
        logits = [sb("logits0", [P, T, LPAD]), sb("logits1", [P, T, E1])]
        left = [sb("left0", [P, T, LPAD]), sb("left1", [P, T, E1])]
        top8 = two("top8", [P, T, 8])
        take3 = sb("take3", [P, T, 8])
        nmx = two("nmx", [P, T])
        chosen = [sb("chosen0", [P, T, E0]), sb("chosen1", [P, T, E1])]
        expl = [sb("expl0", [P, T, E0]), sb("expl1", [P, T, E1])]
        esum = two("esum", [P, T])
        cw = [sb("cw0", [P, T, E0]), sb("cw1", [P, T, E1])]
        CS = two("CS", [P, S], F32R)
        G = [low[0], sb("G1", [P, SLOTS, S])]
        pairs = probs

        ring = [[ctx.enter_context(nc.psum_tensor(f"ring{ph}{s}", [P, 512], F32)) for s in range(RING)]
                for ph in (0, 1)]
        acc = [ctx.enter_context(nc.psum_tensor(f"acc{ph}", [P, 512], F32)) for ph in (0, 1)]

        def sem(name):
            return ctx.enter_context(nc.semaphore(name))

        def signals(name, per0, per1):
            return [Signal(sem(f"{name}{ph}") if per else None, per) for ph, per in ((0, per0), (1, per1))]

        s_res = [sem("resident0"), sem("resident1")]
        s_const = sem("constants")
        s_ready = sem("setup_done")
        s_ones = sem("high_parts_of_b2")
        s_passed = sem("passed_waits")
        full = [[Signal(sem(f"full{ph}{s}"), (USES[ph] - s + RING - 1) // RING) for s in range(RING)]
                for ph in (0, 1)]
        free = [[Signal(sem(f"free{ph}{s}"), (USES[ph] - s + RING - 1) // RING) for s in range(RING)]
                for ph in (0, 1)]
        acc_full = signals("acc_full", 3, 5)
        acc_free = signals("acc_free", 3, 5)
        x_loaded = signals("x_loaded", 16, 0)
        c_loaded = signals("c_loaded", 16, 16)
        var_done = signals("var_done", 2, 8)
        rstd_done = signals("rstd_done", 2, 8)
        xh_done = signals("xh_done", 2, 8)
        affine_done = signals("affine_done", 0, 2)
        x_turned = signals("x_turned", 0, 1)
        hi_done = signals("hi_done", 4, 16)
        q_stacked = signals("q_stacked", 2 * 12 * 16, 2 * 12 * 16)
        k_stacked = signals("k_stacked", 2 * 12 * 16, 2 * 12 * 16)
        mh_done = signals("mh_done", 2, 2)
        m_stacked = signals("m_stacked", 64, 64)
        masked_done = signals("masked_done", 0, 16)
        y0_done = signals("y0_done", 1, 0)
        xs_done = signals("xs_done", 0, 2)
        logits_done = signals("logits_done", 1, 1)
        expl_done = signals("expl_done", 1, 1)
        cw_done = signals("cw_done", 1, 1)
        cs_hi = signals("cs_hi", 1, 1)
        paired = [[Signal(sem(f"paired{ph}{s}"), 16 * ((n // 2 - s + PR - 1) // PR)) for s in range(PR)]
                  for ph, n in ((0, NE0), (1, NE1))]
        pair_used = signals("pair_used", NE0 // 2, NE1 // 2)
        act_done = signals("act_done", E0, NR1)
        stored = Signal(sem("stored"), 16)

        dram_x = x_in.rearrange("b (t p) c -> b p t c", p=P)
        dram_c = ctx_in.rearrange("b (t p) c -> b p t c", p=P)
        dram_o = out.rearrange("b (t p) c -> b p t c", p=P)
        pieces = [pieces0, pieces1]
        NEXP = [NE0, NE1]
        NROUTED = [E0, NR1]
        NEXPERTS = [E0, E1]
        DH = [D0, D1]
        ACC_SUMS = (0, 1, 0, 2)

        def ordinal(ph, a):
            return a - 2 * ph

        def wait_read(eng, ph, b, name, args=(), k=0, before=0):
            r = USE_OF[ph, name, args] + k
            bank_free = free[ph][r % RING]
            eng.wait_ge(bank_free.sem, bank_free.at(b, r // RING + 2 - before * bank_free.per))

        def wait_acc_read(eng, ph, b, n):
            eng.wait_ge(acc_free[ph].sem, acc_free[ph].at(b, n + 2))

        def settle(eng):
            eng.sem_inc(s_passed, 1)

        def drive(eng, steps, setup_l1=None):
            def run(order, **batch):
                for name, ph, r, args in order:
                    b = batch["one"] if ph else batch["head" if (name, args) in HEADS else "tail"]
                    if b is not None and name in steps:
                        steps[name](ph, b, r, *args)

            run(STEPS[0], head=Batch(None, 0), tail=Batch(None, 0))
            if setup_l1:
                setup_l1()
            run(STEPS[0], head=Batch(None, 1), tail=None)
            with eng.Fori(0, NB - 2) as i:
                run(BOTH, one=Batch(i, 0), tail=Batch(i, 1), head=Batch(i, 2))
            run(BOTH, one=Batch(None, NB - 2), tail=Batch(None, NB - 1), head=None)
            run(STEPS[1], one=Batch(None, NB - 1))

        block = ctx.enter_context(nc.Block())

        @block.sync
        def _(sp):
            l1 = COLS["L1"][0]
            sp.dma_start(W[:, 0:l1], resident[:, 0:l1]).then_inc(s_res[0], 16)

            def first(b):
                return b.i is None and b.plus == 0

            def load(ph, b, r):
                i = b.times(1, 0)
                if ph == 0:
                    if not first(b):
                        wait_read(sp, 0, b, "back", (0,), before=1)
                        settle(sp)
                    sp.dma_start(xin[:, :, :], dram_x[i]).then_inc(x_loaded[0].sem, 16)
                    if not first(b):
                        wait_read(sp, 0, b, "turn_context", (1,), before=1)
                        settle(sp)
                else:
                    sp.wait_ge(stored.sem, b.times(16, 16))
                    settle(sp)
                sp.dma_start(ctok[ph][:, :, :], dram_c[i]).then_inc(c_loaded[ph].sem, 16)
                if ph == 0 and first(b):
                    sp.dma_start(W[:, l1:NCOLS], resident[:, l1:NCOLS]).then_inc(s_res[1], 16)

            def stack(ph, b, a, i, terms, to, sig, project, after):
                hi, lo, row, d = parts[a][i]
                if a in (1, 3):
                    wait_read(sp, ph, b, "scores_b", (a - 1, H - 1))
                    settle(sp)
                sp.wait_ge(hi_done[ph].sem, hi_done[ph].at(b, after))
                for part in (hi, lo):
                    if part is lo:
                        wait_read(sp, ph, b, *project, NC - 1)
                    for term in range(3):
                        if terms[term] != (part is lo):
                            continue
                        for j in range(4):
                            dst = to[ph][HR * term:HR * term + d, :, :].rearrange("p (c j) n -> p c j n", j=4)[:, :, j, :]
                            src = part[row + d * j:row + d * (j + 1), :, :]
                            sp.dma_start(dst.bitcast(F32), src.bitcast(F32)).then_inc(sig[ph].sem, 16)

            def stack_q(ph, b, r, a):
                project = ("project_q", (a,)) if ph else ("project_all", ())
                stack(ph, b, a, 0, (0, 0, 1), qs, q_stacked, project, {0: 4, 1: 4, 2: 4, 3: 16}[a])

            def stack_k(ph, b, r, a):
                project = ("project_k", (a,)) if ph else ("project_all", ())
                stack(ph, b, a, 1, (0, 1, 0), ks, k_stacked, project, {0: 4, 1: 4, 2: 8, 3: 12}[a])

            def max_rows(ph, b, r, a):
                sp.wait_ge(mh_done[ph].sem, mh_done[ph].at(b, ordinal(ph, a) + 1))
                sp.dma_start(qs[ph][MROW:MROW + 1, :, :].bitcast(F32), MH[ph][:, :].bitcast(F32)).then_inc(m_stacked[ph].sem, 16)
                wait_read(sp, ph, b, "max_rows", (a,))
                sp.dma_start(qs[ph][MROW + 1:MROW + 2, :, :].bitcast(F32), ML[ph][:, :].bitcast(F32)).then_inc(m_stacked[ph].sem, 16)

            def store(ph, b, r):
                wait_read(sp, 1, b, "back", (4,))
                settle(sp)
                sp.dma_start(dram_o[b.times(1, 0)], result[:, :, :]).then_inc(stored.sem, 16)
                sp.wait_ge(stored.sem, stored.at(b, 32))
                settle(sp)

            sp.sem_inc(stored.sem, 16)
            drive(sp, dict(load=load, stack_q=stack_q, stack_k=stack_k, max_rows=max_rows, store=store))

        @block.gpsimd
        def _(pool):
            def select(tile, src, op, fill, base):
                return pool.affine_select(out=tile[:, :], in_=src[:, :], compare_op=op, fill=fill, base=base,
                                          pattern=[[-1, P]], channel_multiplier=1)
            pool.memset(ident[:, :], 0.0)
            pool.memset(zerosb[:, :], 0.0)
            pool.memset(minus_half[:, :], -0.5)
            pool.drain()
            select(ident, ident, ALU.not_equal, 1.0, 0)
            select(mask_qk, zerosb, ALU.is_ge, NEG, 0)
            pool.affine_select(out=mask_kq[:, :], in_=zerosb[:, :], compare_op=ALU.is_ge, fill=NEG, base=0,
                               pattern=[[1, P]], channel_multiplier=-1)
            pool.drain()
            pool.tensor_copy(identb[:, :], ident[:, :]).then_inc(s_const, 1)
            pool.memset(ks[0][0:KROWS, :, :].bitcast(F32), 0.0)
            pool.drain()
            for ph in (0, 1):
                pool.memset(ks[ph][KROWS:P, :, :].bitcast(F32), 1.0)
            pool.drain()
            for ph in (0, 1):
                pool.memset(CS[ph][:, :].bitcast(F32), 0.0)
                pool.memset(cT[ph][:, :], 0.0)
            pool.drain()
            pool.sem_inc(s_const, 1)
            pool.wait_ge(s_ready, 2)

            def ln_stats(ph, b, r, i):
                pool.wait_ge(var_done[ph].sem, var_done[ph].at(b, i + 1))
                pool.tensor_tensor(rstd[ph][:, :], ve[ph][:, :], minus_half[:, :], ALU.pow).then_inc(rstd_done[ph].sem, 1)

            def affine(ph, b, r, i):
                g, beta = (("ln1g", "ln1b"), ("ln2g", "ln2b"))[i]
                pool.wait_ge(xh_done[1].sem, xh_done[1].at(b, (1, 5)[i]))
                rows = lambda name: col(name).unsqueeze(1).to_broadcast([P, T, C])
                pool.tensor_tensor(scaled[:, :, :], xh[1][:, :, :], rows(g), ALU.mult)
                pool.drain()
                pool.tensor_tensor(X1[:, :, :], scaled[:, :, :], rows(beta), ALU.add).then_inc(affine_done[1].sem, 1)

            def scores_b(ph, b, r, a, h):
                if a != 2:
                    return
                wait_read(pool, 1, b, "scores_b", (2, h))
                settle(pool)
                view = probs[1][:, h % PR, :].rearrange("p (a n) -> p a n", a=4)[:, 0:4:3, :]
                pool.affine_select(out=masked[:, h % PR, :, :], in_=view, compare_op=ALU.is_gt, fill=0.0, base=0,
                                   pattern=[[0, 2], [-1, P]], channel_multiplier=1).then_inc(masked_done[1].sem, 1)

            def back(ph, b, r, n):
                if ph == 0 or n not in (0, 2):
                    return
                wait_read(pool, 1, b, "back", (n,))
                settle(pool)
                if n == 0:
                    pool.tensor_tensor(XS[:, :, :], XO[:, :, :], X1[:, :, :], ALU.add).then_inc(xs_done[1].sem, 1)
                else:
                    pool.tensor_tensor(scaled[:, :, :], XO[:, :, :], X1[:, :, :], ALU.add)
                    pool.drain()
                    pool.tensor_tensor(XS[:, :, :], scaled[:, :, :], X0[:, :, :], ALU.add).then_inc(xs_done[1].sem, 1)

            def bring(ph, g):
                dst = pairs[ph][:, g % PR, :].rearrange("p (e n) -> p e n", e=2)
                pool.dma_start(dst, pieces[ph][:, 2 * g:2 * g + 2, :]).then_inc(paired[ph][g % PR].sem, 16)

            def load_experts(ph, b, r, a):
                pool.wait_ge(acc_full[ph].sem, acc_full[ph].at(b, ACC_SUMS[a] + 1))
                settle(pool)
                for g in range(PR):
                    bring(ph, g)

            def reload(ph, b, g):
                if g + PR < NEXP[ph] // 2:
                    pool.wait_ge(pair_used[ph].sem, pair_used[ph].at(b, g + 1))
                    settle(pool)
                    bring(ph, g + PR)

            def expert(ph, b, r, e):
                if e >= LAG + 1 and (e - LAG) % 2 == 1:
                    reload(ph, b, (e - LAG) // 2)

            def setup_l1():
                pool.wait_ge(s_res[1], 16)

            drive(pool, dict(ln_stats=ln_stats, affine=affine, scores_b=scores_b, back=back, load_experts=load_experts, expert=expert), setup_l1)

        @block.tensor
        def _(pe):
            pe.wait_ge(s_const, 2)
            pe.wait_ge(s_ready, 2)
            pe.wait_ge(s_res[0], 16)

            def begin(ph, b, r):
                s = r % RING
                pe.wait_ge(free[ph][s].sem, free[ph][s].at(b, r // RING + 1))
                return ring[ph][s]

            def begin_acc(ph, b, n):
                pe.wait_ge(acc_free[ph].sem, acc_free[ph].at(b, n + 1))
                return acc[ph]

            def end(ph, r, ins):
                ins.then_inc(full[ph][r % RING].sem, 1)

            def turn_tile(ph, b, r, tile, width):
                bank = begin(ph, b, r)
                settle(pe)
                for t in range(T):
                    ins = pe.transpose(bank[0:width, t * P:(t + 1) * P], tile[:, t, 0:width], ident[:, :])
                end(ph, r, ins)

            def turn(ph, b, r, n):
                which = {(0, 0): 1, (0, 2): 2, (1, 1): 4, (1, 2): 6, (1, 4): 7, (1, 5): 8}[ph, n]
                pe.wait_ge(xh_done[ph].sem, xh_done[ph].at(b, which))
                turn_tile(ph, b, r, xh[ph], C)

            def turn_two(ph, b, r, n):
                pe.wait_ge(xh_done[1].sem, xh_done[1].at(b, 2))
                turn_tile(1, b, r, xh[1], C)

            def turn_context(ph, b, r, n):
                if ph == 0:
                    pe.wait_ge(c_loaded[0].sem, c_loaded[0].at(b, 16))
                    turn_tile(0, b, r, ctok[0], CC)
                else:
                    pe.wait_ge(xh_done[1].sem, xh_done[1].at(b, 3))
                    turn_tile(1, b, r, xh[1], CC)

            def project(b, r, weight, src):
                for c in range(NC):
                    bank = begin(1, b, r + c)
                    end(1, r + c, pe.matmul(bank[:, 0:S], col(weight, c * P, P), src[:, :], start=True, stop=True))

            def project_all(ph, b, r):
                wait_read(pe, 0, b, "turn", (0,))
                for c in range(NC):
                    bank = begin(0, b, r + c)
                    pe.matmul(bank[0:96, 0:S], col("wqkq", c * 96, 96), xT[0][:, :], start=True, stop=True)
                    end(0, r + c, pe.matmul(bank[96:P, 0:S], col("wk1", c * 32, 32), cT[0][:, :], start=True, stop=True,
                                            tile_position=(0, 96), skip_group_check=True))

            def project_values(ph, b, r):
                for t in range(T):
                    bank = begin(0, b, r + t)
                    pe.matmul(bank[:, 0:C], xT[0][:, t * P:(t + 1) * P], col("wv0"), start=True, stop=True)
                    end(0, r + t, pe.matmul(bank[:, C:2 * C], cT[0][:, t * P:(t + 1) * P], col("wv1"), start=True, stop=True))

            def project_q(ph, b, r, a):
                wait_read(pe, 1, b, *{2: ("turn_two", (0,)), 3: ("turn", (2,))}[a])
                project(b, r, f"wq{a}", xT[1])

            def key_source(a):
                return yT if a == 2 else cT[1]

            def project_k(ph, b, r, a):
                if a == 3:
                    wait_read(pe, 1, b, "turn_context", (3,))
                project(b, r, f"wk{a}", key_source(a))

            def project_v(ph, b, r, a):
                for t in range(T):
                    bank = begin(1, b, r + t)
                    end(1, r + t, pe.matmul(bank[:, :], key_source(a)[:, t * P:(t + 1) * P], col(f"wv{a}"), start=True, stop=True))

            def scores_a(ph, b, r, a, h):
                n = ordinal(ph, a) + 1
                if h == 0:
                    pe.wait_ge(q_stacked[ph].sem, q_stacked[ph].at(b, 192 * n))
                    pe.wait_ge(k_stacked[ph].sem, k_stacked[ph].at(b, 192 * n))
                bank = begin(ph, b, r)
                for t in range(T):
                    keys = P if a == 0 and t == 0 else S
                    ins = pe.matmul(bank[:, t * S:t * S + keys], qs[ph][0:KROWS, h, t * P:(t + 1) * P],
                                    ks[ph][0:KROWS, h, 0:keys], start=True, stop=True)
                    if a == 0:
                        ins = pe.matmul(bank[:, t * S + t * P:t * S + (t + 1) * P], identb[:, :], mask_qk[:, :],
                                        start=False, stop=True, skip_group_check=True)
                end(ph, r, ins)

            def max_rows(ph, b, r, a):
                wait_read(pe, ph, b, "scores_a", (a, H - 1))
                bank = begin(ph, b, r)
                for t in range(T):
                    ins = pe.transpose(bank[0:H, t * P:(t + 1) * P], negmax[ph][:, t, :], ident[:, :])
                end(ph, r, ins)

            def scores_b(ph, b, r, a, h):
                if h == 0:
                    pe.wait_ge(m_stacked[ph].sem, m_stacked[ph].at(b, 32 * (ordinal(ph, a) + 1)))
                bank = begin(ph, b, r)
                for t in range(T):
                    q0 = t * P if a == 0 else 0
                    ins = pe.matmul(bank[:, t * S + q0:(t + 1) * S], ks[ph][0:MROW + 2, h, t * P:(t + 1) * P],
                                    qs[ph][0:MROW + 2, h, q0:S], start=True, stop=True)
                    if a == 0:
                        ins = pe.matmul(bank[:, t * S + q0:t * S + q0 + P], identb[:, :], mask_kq[:, :],
                                        start=False, stop=True, skip_group_check=True)
                end(ph, r, ins)

            def values(ph, b, r, a, c):
                n = ordinal(ph, a)
                wait_read(pe, ph, b, "scores_b", (a, 4 * c + 3))
                if c == 0:
                    wait_read(pe, ph, b, *(("project_v", (a,)) if ph else ("project_values", ())), T - 1)
                    begin_acc(ph, b, ACC_SUMS[a])
                if a == 2:
                    pe.wait_ge(masked_done[1].sem, masked_done[1].at(b, 4 * c + 4))
                bank = begin(ph, b, r)

                def product(j, t, q0, q1, rhs, start, stop):
                    h = 4 * c + j
                    v = V[1][:, t, HR * h:HR * (h + 1)] if ph else V[0][:, t, C * n + HR * c:C * n + HR * (c + 1)]
                    return pe.matmul(bank[HR * j:HR * (j + 1), q0:q1], v, rhs,
                                     start=start, stop=stop, tile_position=(0, HR * j), skip_group_check=True)

                def prob(j, t, q0, q1):
                    return probs[ph][:, (4 * c + j) % PR, t * S + q0:t * S + q1]

                if a == 2:
                    for j in range(4):
                        product(j, 1, P, S, masked[:, (4 * c + j) % PR, 1, :], True, True)
                    for j in range(4):
                        product(j, 0, 0, P, masked[:, (4 * c + j) % PR, 0, :], True, False)
                    for j in range(4):
                        ins = product(j, 1, 0, P, prob(j, 1, 0, P), False, True)
                else:
                    for t in range(T):
                        q0 = t * P if a == 0 else 0
                        for j in range(4):
                            ins = product(j, t, q0, S, prob(j, t, q0, S), t == 0, t == T - 1)
                end(ph, r, ins)
                for t in range(T):
                    q0 = t * P if a == 0 else 0
                    for j in range(4):
                        ins = pe.matmul(acc[ph][HR * j:HR * (j + 1), q0:S], sum_lhs[:, c, :], prob(j, t, q0, S),
                                        start=c == 0 and t == 0, stop=c == NC - 1 and t == T - 1,
                                        tile_position=(0, HR * j), skip_group_check=True)
                if c == NC - 1:
                    ins.then_inc(acc_full[ph].sem, 1)

            def normalize(ph, b, r, a):
                wait_acc_read(pe, ph, b, ACC_SUMS[a])
                for c in range(NC):
                    bank = begin(ph, b, r + c)
                    lhs = spread[:, c, :, :].rearrange("p j d -> p (j d)")
                    end(ph, r + c, pe.matmul(bank[:, 0:S], lhs, R[ph][:, :], start=True, stop=True))

            def out_project(ph, b, r, a, n):
                src, weight = {0: (Y0, "wp"), 2: (O[1], "li1_2"), 3: (O[1], "li1_3")}[a]
                if ph == 0:
                    pe.wait_ge(y0_done[0].sem, y0_done[0].at(b, 1))
                else:
                    wait_read(pe, 1, b, "normalize", (a,), NC - 1)
                bank = begin(ph, b, r)
                for c in range(NC):
                    ins = pe.matmul(bank[:, 0:S], col(weight, c * C, C), src[:, c, :], start=c == 0, stop=c == NC - 1)
                end(ph, r, ins)

            def back(ph, b, r, n):
                made_by = {(0, 0): (0, 0), (1, 0): (2, 0), (1, 2): (3, 2)}.get((ph, n))
                if made_by:
                    wait_read(pe, ph, b, "out_project", made_by)
                else:
                    wait_acc_read(pe, ph, b, {(0, 1): 2, (1, 1): 1, (1, 3): 3, (1, 4): 4}[ph, n])
                bank = begin(ph, b, r)
                for t in range(T):
                    ins = pe.transpose(bank[:, t * C:(t + 1) * C], F[ph][:, t * P:(t + 1) * P], ident[:, :])
                end(ph, r, ins)

            def mlp(ph, b, r, m, n):
                wait_read(pe, 1, b, "turn", ((1, 4)[m],))
                project(b, r, f"li2_{m + 2}", xT[1])

            def mlp_out(ph, b, r, m, n):
                bank = begin_acc(1, b, (1, 3)[m])
                for c in range(NC):
                    wait_read(pe, 1, b, "mlp", (m, n), c)
                    ins = pe.matmul(bank[:, 0:S], col(f"li3_{m + 2}", c * C, C), hidden[:, c, :], start=c == 0, stop=c == NC - 1)
                ins.then_inc(acc_full[1].sem, 1)

            def router(ph, b, r):
                wait_read(pe, ph, b, "turn", ((2, 5)[ph],))
                bank = begin(ph, b, r)
                ne = NEXPERTS[ph]
                for t in range(T):
                    ins = pe.matmul(bank[:, t * ne:(t + 1) * ne], xT[ph][:, t * P:(t + 1) * P], col(f"rw{ph}"), start=True, stop=True)
                end(ph, r, ins)

            def turn_weights(ph, b, r):
                pe.wait_ge(cw_done[ph].sem, cw_done[ph].at(b, 1))
                turn_tile(ph, b, r, cw[ph], NEXPERTS[ph])

            def weights(ph, e):
                return pairs[ph][:, e // 2 % PR, 2 * C * (e % 2):2 * C * (e % 2 + 1)]

            def expert_sum(ph, b, e):
                wait_read(pe, ph, b, "expert", (e,))
                ins = pe.matmul(acc[ph][:, 0:S], weights(ph, e)[:, C:2 * C], G[ph][:, e % SLOTS, :], start=False,
                                stop=e == NEXP[ph] - 1)
                if e % 2 == 1:
                    ins.then_inc(pair_used[ph].sem, 1)

            def expert(ph, b, r, e):
                if e == 0:
                    wait_read(pe, ph, b, "turn_weights")
                    bank = begin_acc(ph, b, (2, 4)[ph])
                    pe.matmul(bank[:, 0:S], b2hi[ph][:, :], CS[ph][:, :], start=True, stop=False)
                    pe.matmul(bank[:, 0:S], b2lo[ph][:, :], CS[ph][:, :], start=False, stop=False)
                if e % 2 == 0:
                    pair = paired[ph][e // 2 % PR]
                    pe.wait_ge(pair.sem, pair.at(b, 16 * (e // (2 * PR) + 1)))
                bank = begin(ph, b, r)
                ins = pe.matmul(bank[:, 0:S], weights(ph, e)[:, 0:C], xT[ph][:, :], start=True, stop=True)
                if e < NROUTED[ph]:
                    if ph == 0:
                        lhs = pick0[:, e:e + 1].to_broadcast([P, P])
                    else:
                        lhs = pick1[:, 4 * e:4 * e + 4, :].rearrange("p e d -> p (e d)")
                    ins = pe.matmul(bank[:, S:2 * S], lhs, CS[ph][:, :], start=True, stop=True)
                end(ph, r, ins)
                if e >= LAG:
                    expert_sum(ph, b, e - LAG)

            def expert_last(ph, b, r, n):
                for e in range(NEXP[ph] - LAG, NEXP[ph]):
                    expert_sum(ph, b, e)
                pe.wait_ge(pair_used[ph].sem, pair_used[ph].at(b, NEXP[ph] // 2))
                pe.sem_inc(acc_full[ph].sem, 1)

            def even_out(ph, b, r):
                for k in range(USES[ph] - r):
                    begin(ph, b, r + k)
                    pe.sem_inc(full[ph][(r + k) % RING].sem, 1)

            def setup_l1():
                pe.wait_ge(s_res[1], 16)
                pe.wait_ge(s_ready, 3)

            drive(pe, dict(even_out=even_out, project_all=project_all, project_values=project_values, turn=turn, turn_two=turn_two, turn_context=turn_context, project_q=project_q, project_k=project_k,
                           project_v=project_v, scores_a=scores_a, max_rows=max_rows, scores_b=scores_b, values=values,
                           normalize=normalize, out_project=out_project, back=back, mlp=mlp, mlp_out=mlp_out, router=router,
                           turn_weights=turn_weights, expert=expert, expert_last=expert_last), setup_l1)

        @block.scalar
        def _(act):
            act.wait_ge(s_res[0], 16)
            act.activation(b2hi[0][:, :], col("eb2"), ACT.Copy).then_inc(s_ones, 1)
            act.wait_ge(s_const, 2)
            act.wait_ge(s_ready, 2)

            def read(ph, b, r):
                s = r % RING
                act.wait_ge(full[ph][s].sem, full[ph][s].at(b, r // RING + 1))
                return ring[ph][s]

            def release(ph, r, ins):
                ins.then_inc(free[ph][r % RING].sem, 1)

            def turn(ph, b, r, n):
                bank = read(ph, b, r)
                aff = {(1, 1): ("g3_2", "b3_2"), (1, 2): ("gx_3", "bx_3"), (1, 4): ("g3_3", "b3_3")}.get((ph, n))
                if aff:
                    ins = act.activation(xT[ph][:, :], bank[:, 0:S], ACT.Identity, bias=col(aff[1]), scale=col(aff[0]))
                else:
                    ins = act.activation(xT[ph][:, :], bank[:, 0:S], ACT.Copy)
                release(ph, r, ins)

            def turn_two(ph, b, r, n):
                bank = read(1, b, r)
                act.activation(xT[1][:, :], bank[:, 0:S], ACT.Identity, bias=col("bx_2"), scale=col("gx_2")).then_inc(x_turned[1].sem, 1)

            def turn_context(ph, b, r, n):
                bank = read(ph, b, r)
                if ph == 0:
                    ins = act.activation(cT[0][0:CC, :], bank[0:CC, 0:S], ACT.Copy)
                else:
                    ins = act.activation(cT[1][0:CC, :], bank[0:CC, 0:S], ACT.Identity, bias=col("by_3")[0:CC], scale=col("gy_3")[0:CC])
                release(ph, r, ins)

            def project_all(ph, b, r):
                for c in range(NC):
                    bank = read(0, b, r + c)
                    act.activation(high0[:, c, :], bank[:, 0:S], ACT.Identity, bias=col("bqkqk", c, 1)).then_inc(hi_done[0].sem, 1)

            def high_parts(b, r, a, i):
                for c in range(NC):
                    bank = read(1, b, r + c)
                    act.activation(parts[a][i][0][:, c, :], bank[:, 0:S], ACT.Copy).then_inc(hi_done[1].sem, 1)

            def project_q(ph, b, r, a):
                high_parts(b, r, a, 0)

            def project_k(ph, b, r, a):
                high_parts(b, r, a, 1)

            def project_values(ph, b, r):
                for t in range(T):
                    bank = read(0, b, r + t)
                    release(0, r + t, act.activation(V[0][:, t, :], bank[:, 0:2 * C], ACT.Copy))

            def project_v(ph, b, r, a):
                for t in range(T):
                    bank = read(1, b, r + t)
                    release(1, r + t, act.activation(V[1][:, t, :], bank[:, :], ACT.Copy))

            def max_rows(ph, b, r, a):
                bank = read(ph, b, r)
                act.activation(MH[ph][:, :], bank[0:H, 0:S], ACT.Copy).then_inc(mh_done[ph].sem, 1)

            def scores_b(ph, b, r, a, h):
                bank = read(ph, b, r)
                scale = float(DH[ph]) ** -0.5
                if a == 0:
                    act.activation(probs[ph][:, h % PR, 0:S], bank[:, 0:S], ACT.Exp, scale=scale)
                    ins = act.activation(probs[ph][:, h % PR, S + P:2 * S], bank[:, S + P:2 * S], ACT.Exp, scale=scale)
                else:
                    ins = act.activation(probs[ph][:, h % PR, :], bank[:, :], ACT.Exp, scale=scale)
                release(ph, r, ins)

            def values(ph, b, r, a, c):
                bank = read(ph, b, r)
                ins = act.activation(attended[a][:, c, :], bank[:, 0:S], ACT.Copy)
                release(ph, r, ins)

            def feature_result(ph, src, bias):
                return act.activation(F[ph][:, :], src, ACT.Identity, bias=bias)

            def out_project(ph, b, r, a, n):
                bank = read(ph, b, r)
                ins = feature_result(ph, bank[:, 0:S], col({0: "bp", 2: "li1b_2", 3: "li1b_3"}[a]))
                release(ph, r, ins)

            def acc_result(ph, b, n, bias):
                act.wait_ge(acc_full[ph].sem, acc_full[ph].at(b, n + 1))
                feature_result(ph, acc[ph][:, 0:S], bias).then_inc(acc_free[ph].sem, 1)

            def mlp(ph, b, r, m, n):
                if m == 0:
                    act.wait_ge(k_stacked[1].sem, k_stacked[1].at(b, 384))
                for c in range(NC):
                    bank = read(1, b, r + c)
                    ins = act.activation(hidden[:, c, :], bank[:, 0:S], ACT.Gelu, bias=col(f"li2b_{m + 2}", c, 1))
                    release(1, r + c, ins)

            def mlp_out(ph, b, r, m, n):
                acc_result(1, b, (1, 3)[m], col(f"li3b_{m + 2}"))

            def router(ph, b, r):
                act.wait_ge(logits_done[ph].sem, logits_done[ph].at(b, 1))
                for t in range(T):
                    ins = act.activation(expl[ph][:, t, :], logits[ph][:, t, 0:NEXPERTS[ph]], ACT.Exp, bias=nmx[ph][:, t:t + 1],
                                         accum_out=esum[ph][:, t:t + 1])
                ins.then_inc(expl_done[ph].sem, 1)

            def turn_weights(ph, b, r):
                bank = read(ph, b, r)
                ne = NEXPERTS[ph]
                act.activation(CS[ph][0:ne, :], bank[0:ne, 0:S], ACT.Copy).then_inc(cs_hi[ph].sem, 1)

            def expert(ph, b, r, e):
                bank = read(ph, b, r)
                f, bias = (ACT.Relu, "eb1") if ph == 0 else (ACT.Silu, "fb1")
                ins = act.activation(G[ph][:, e % SLOTS, :], bank[:, 0:S], f, bias=col(bias, e, 1))
                if e < NROUTED[ph]:
                    ins.then_inc(act_done[ph].sem, 1)
                else:
                    release(ph, r, ins)

            def expert_last(ph, b, r, n):
                acc_result(ph, b, (2, 4)[ph], col("sb2") if ph == 0 else fsb2_sum[:, :])

            def setup_l1():
                act.wait_ge(s_res[1], 16)
                act.activation(b2hi[1][:, :], col("fb2"), ACT.Copy).then_inc(s_ones, 1)
                act.wait_ge(s_ready, 3)

            drive(act, dict(project_all=project_all, project_values=project_values, turn=turn, turn_two=turn_two, turn_context=turn_context, project_q=project_q, project_k=project_k,
                            project_v=project_v, max_rows=max_rows, scores_b=scores_b, values=values, out_project=out_project,
                            mlp=mlp, mlp_out=mlp_out, router=router, turn_weights=turn_weights, expert=expert,
                            expert_last=expert_last), setup_l1)

        @block.vector
        def _(dve):
            dve.memset(sum_lhs[:, :, :], 1.0)
            dve.drain()
            dve.memset(sum_lhs[:, :, 0:NC], 0.0)
            dve.memset(logits[0][:, :, :], SENT)
            dve.memset(take3[:, :, :], SENT)
            dve.memset(qs[0][:, :, :].bitcast(F32), 0.0)
            dve.drain()
            for c in range(NC):
                dve.memset(sum_lhs[:, c, c:c + 1], 1.0)
            for ph in (0, 1):
                for s in range(RING):
                    dve.memset(ring[ph][s][:, :], 0.0).then_inc(free[ph][s].sem, 1)
                dve.memset(acc[ph][:, :], 1.0).then_inc(acc_free[ph].sem, 1)
            dve.wait_ge(s_const, 1)
            dve.tensor_tensor(pick0[:, :], ident[:, 0:E0], ident[:, 32:32 + E0], ALU.add)
            wide = lambda at: ident[:, at:at + E1].unsqueeze(2).to_broadcast([P, E1, HR])
            dve.tensor_tensor(pick1[:, :, :], wide(0), wide(E1), ALU.add)
            for c in range(NC):
                dve.tensor_copy(spread[:, c, :, :], ident[:, c:P:HR].unsqueeze(2).to_broadcast([P, 4, HR]))
            dve.wait_ge(s_res[0], 16)
            dve.tensor_tensor(bv_sum[:, :], col("bv0"), col("bv1"), ALU.add)
            dve.wait_ge(s_ones, 1)
            dve.tensor_tensor(b2lo[0][:, :], col("eb2"), b2hi[0][:, :].bitcast(F32), ALU.subtract)
            dve.drain()
            dve.sem_inc(s_ready, 2)
            dve.wait_ge(s_const, 2)

            def read(ph, b, r):
                s = r % RING
                dve.wait_ge(full[ph][s].sem, full[ph][s].at(b, r // RING + 1))
                return ring[ph][s]

            def release(ph, r, ins):
                ins.then_inc(free[ph][r % RING].sem, 1)

            def ln_source(ph, i):
                return {(0, 0): xin, (0, 1): x1, (1, 0): handed, (1, 1): X1, (1, 2): ctok[1], (1, 3): XO, (1, 4): XS,
                        (1, 5): X1, (1, 6): XO, (1, 7): XS}[ph, i]

            def ln_width(ph, i):
                return CC if (ph, i) == (1, 2) else C

            def ln_stats(ph, b, r, i):
                dve.drain()
                if (ph, i) == (0, 0):
                    dve.wait_ge(x_loaded[0].sem, x_loaded[0].at(b, 16))
                if (ph, i) in ((1, 1), (1, 5)):
                    dve.wait_ge(affine_done[1].sem, affine_done[1].at(b, {1: 1, 5: 2}[i]))
                if (ph, i) == (1, 2):
                    dve.wait_ge(c_loaded[1].sem, c_loaded[1].at(b, 16))
                src, w = ln_source(ph, i), ln_width(ph, i)
                for t in range(T):
                    dve.bn_stats(stats[ph][:, t, :], src[:, t, 0:w])
                dve.drain()
                for t in range(T):
                    dve.bn_aggr(mv[ph][:, t, :], stats[ph][:, t, :])
                dve.drain()
                if (ph, i) == (1, 0):
                    ins = dve.tensor_scalar(ve[1][:, :], mv[1][:, :, 1], 1.0 + EPS, EPS * EPS, ALU.mult, ALU.add)
                else:
                    ins = dve.tensor_scalar(ve[ph][:, :], mv[ph][:, :, 1], EPS, None, ALU.add)
                ins.then_inc(var_done[ph].sem, 1)

            def ln_apply(ph, b, r, i):
                src, w = ln_source(ph, i), ln_width(ph, i)
                dve.wait_ge(rstd_done[ph].sem, rstd_done[ph].at(b, i + 1))
                for t in range(T):
                    ins = dve.tensor_scalar(xh[ph][:, t, 0:w], src[:, t, 0:w], mv[ph][:, t, 0:1], rstd[ph][:, t:t + 1],
                                            ALU.subtract, ALU.mult)
                ins.then_inc(xh_done[ph].sem, 1)

            def take(ph, b, r):
                dve.drain()
                dve.tensor_copy(X0[:, :, :], handed[:, :, :])

            def turn_two(ph, b, r, n):
                bank = read(1, b, r)
                dve.wait_ge(x_turned[1].sem, x_turned[1].at(b, 1))
                ins = dve.tensor_scalar(yT[:, :], bank[:, 0:S], col("gy_2"), col("by_2"), ALU.mult, ALU.add)
                release(1, r, ins)

            def project_all(ph, b, r):
                for c in range(NC):
                    bank = read(0, b, r + c)
                    dve.wait_ge(hi_done[0].sem, hi_done[0].at(b, c + 1))
                    release(0, r + c, dve.scalar_tensor_tensor(parts[0][0][1][:, c, :], bank[:, 0:S], col("bqkqk", c, 1),
                                                               high0[:, c, :].bitcast(F32), ALU.add, ALU.subtract))

            def low_parts(b, r, a, i, done):
                hi, lo = parts[a][i][:2]
                for c in range(NC):
                    bank = read(1, b, r + c)
                    dve.wait_ge(hi_done[1].sem, hi_done[1].at(b, done + c + 1))
                    release(1, r + c, dve.tensor_tensor(lo[:, c, :], bank[:, 0:S], hi[:, c, :].bitcast(F32), ALU.subtract))

            def project_q(ph, b, r, a):
                low_parts(b, r, a, 0, {2: 0, 3: 12}[a])

            def project_k(ph, b, r, a):
                low_parts(b, r, a, 1, {2: 4, 3: 8}[a])

            def scores_a(ph, b, r, a, h):
                bank = read(ph, b, r)
                if a == 0:
                    dve.tensor_reduce(negmax[ph][:, 0, h:h + 1], bank[:, 0:P], AX.X, ALU.max, negate=True)
                    ins = dve.tensor_reduce(negmax[ph][:, 1, h:h + 1], bank[:, S:2 * S], AX.X, ALU.max, negate=True)
                else:
                    ins = dve.tensor_reduce(negmax[ph][:, :, h], bank[:, :].rearrange("p (t n) -> p t n", t=T), AX.X, ALU.max, negate=True)
                release(ph, r, ins)

            def max_rows(ph, b, r, a):
                bank = read(ph, b, r)
                dve.wait_ge(mh_done[ph].sem, mh_done[ph].at(b, ordinal(ph, a) + 1))
                ins = dve.tensor_tensor(ML[ph][:, :], bank[0:H, 0:S], MH[ph][:, :].bitcast(F32), ALU.subtract)
                release(ph, r, ins)

            def sums(ph, b, r, a):
                dve.wait_ge(acc_full[ph].sem, acc_full[ph].at(b, ACC_SUMS[a] + 1))
                dve.reciprocal(R[ph][:, :], acc[ph][:, 0:S]).then_inc(acc_free[ph].sem, 1)

            def normalize(ph, b, r, a):
                wait_read(dve, ph, b, "values", (a, NC - 1))
                for c in range(NC):
                    bank = read(ph, b, r + c)
                    ins = dve.tensor_tensor(attended[a][:, c, :], bank[:, 0:S], attended[a][:, c, :], ALU.mult)
                    release(ph, r + c, ins)
                if a == 1:
                    dve.drain()
                    for c in range(NC):
                        ins = dve.scalar_tensor_tensor(Y0[:, c, :], O[0][:, c, :], bv_sum[:, c:c + 1], Y0[:, c, :], ALU.add, ALU.add)
                    ins.then_inc(y0_done[0].sem, 1)

            def back(ph, b, r, n):
                bank = read(ph, b, r)
                dst, other = {(0, 0): (x1, xin), (0, 1): (handed, x1), (1, 0): (XO, X1), (1, 1): (XS, XS), (1, 2): (XO, X1),
                              (1, 3): (XS, XS), (1, 4): (result, XS)}[ph, n]
                if (ph, n) in ((1, 1), (1, 3)):
                    dve.wait_ge(xs_done[1].sem, xs_done[1].at(b, (n + 1) // 2))
                flat = lambda tile: tile[:, :, :].rearrange("p t c -> p (t c)")
                ins = dve.tensor_tensor(flat(dst), bank[:, 0:T * C], flat(other), ALU.add)
                release(ph, r, ins)

            def router(ph, b, r):
                bank = read(ph, b, r)
                ne = NEXPERTS[ph]
                rb = col(f"rb{ph}").unsqueeze(1).to_broadcast([P, T, ne])
                ins = dve.tensor_tensor(logits[ph][:, :, 0:ne], bank[:, 0:T * ne].rearrange("p (t e) -> p t e", t=T), rb, ALU.add)
                release(ph, r, ins)
                dve.drain()
                for t in range(T):
                    dve.max(top8[ph][:, t, :], logits[ph][:, t, :])
                dve.drain()
                dve.tensor_scalar(nmx[ph][:, :], top8[ph][:, :, 0], -1.0, None, ALU.mult).then_inc(logits_done[ph].sem, 1)
                found = top8[1]
                if ph == 0:
                    dve.tensor_copy(take3[:, :, 0:K0], top8[0][:, :, 0:K0])
                    dve.drain()
                    found = take3
                for t in range(T):
                    dve.match_replace(left[ph][:, t, :], found[:, t, :], logits[ph][:, t, :], TAKEN)
                dve.drain()
                dve.tensor_tensor(chosen[ph][:, :, :], left[ph][:, :, 0:ne], logits[ph][:, :, 0:ne], ALU.not_equal)
                dve.drain()
                dve.wait_ge(expl_done[ph].sem, expl_done[ph].at(b, 1))
                if ph == 1:
                    dve.tensor_tensor(expl[1][:, :, :], expl[1][:, :, :], chosen[1][:, :, :], ALU.mult)
                    dve.drain()
                    dve.tensor_reduce(esum[1][:, :], expl[1][:, :, :], AX.X, ALU.add)
                    dve.drain()
                dve.reciprocal(esum[ph][:, :], esum[ph][:, :])
                dve.drain()
                for t in range(T):
                    ins = dve.scalar_tensor_tensor(cw[ph][:, t, :], expl[ph][:, t, :], esum[ph][:, t:t + 1], chosen[ph][:, t, :],
                                                   ALU.mult, ALU.mult)
                ins.then_inc(cw_done[ph].sem, 1)

            def turn_weights(ph, b, r):
                bank = read(ph, b, r)
                ne, at = NEXPERTS[ph], (32, 64)[ph]
                dve.wait_ge(cs_hi[ph].sem, cs_hi[ph].at(b, 1))
                ins = dve.tensor_tensor(CS[ph][at:at + ne, :], bank[0:ne, 0:S], CS[ph][0:ne, :].bitcast(F32), ALU.subtract)
                release(ph, r, ins)

            def expert(ph, b, r, e):
                if e >= NROUTED[ph]:
                    return
                bank = read(ph, b, r)
                dve.wait_ge(act_done[ph].sem, act_done[ph].at(b, e + 1))
                release(ph, r, dve.tensor_tensor(G[ph][:, e % SLOTS, :], bank[:, S:2 * S], G[ph][:, e % SLOTS, :], ALU.mult))

            def even_out(ph, b, r):
                for k in range(USES[ph] - r):
                    read(ph, b, r + k)
                    dve.sem_inc(free[ph][(r + k) % RING].sem, 1)

            def setup_l1():
                dve.wait_ge(s_res[1], 16)
                dve.wait_ge(s_ones, 2)
                dve.tensor_tensor(fsb2_sum[:, :], col("fsb2", 0, 1), col("fsb2", 1, 1), ALU.add)
                dve.tensor_tensor(b2lo[1][:, :], col("fb2"), b2hi[1][:, :].bitcast(F32), ALU.subtract).then_inc(s_ready, 1)

            drive(dve, dict(even_out=even_out, project_all=project_all, ln_stats=ln_stats, ln_apply=ln_apply, take=take, turn_two=turn_two, project_q=project_q,
                            project_k=project_k, scores_a=scores_a, max_rows=max_rows, sums=sums, normalize=normalize, back=back,
                            router=router, turn_weights=turn_weights, expert=expert), setup_l1)


def _pad_rows(a):
    return np.concatenate([a, np.zeros((P - a.shape[0],) + a.shape[1:], a.dtype)]) if a.shape[0] < P else a


def _head_vector(v):
    out = np.zeros((NC, 4, 4, D0), v.dtype)
    for j in range(4):
        out[:, j, j, :] = v.reshape(NC, 4, D0)[:, j]
    return out.reshape(NC, P).T


def _chunk_rows(w):
    return w.reshape(-1, P, w.shape[1]).transpose(1, 0, 2).reshape(P, -1)


def _row_everywhere(v):
    return np.broadcast_to(v[None, :], (P, v.shape[0]))


def lay_out(a):
    L0 = lambda n: a["L0_xattn_" + n]
    L1 = lambda n: a["L1_xattn_" + n]
    cols = {"L1": np.zeros((P, 0), np.float32)}
    by_chunk = lambda n: L0(n).reshape(C, NC, 4 * D0)
    cols["wqkq"] = np.concatenate([by_chunk("Wq"), by_chunk("Wk"), by_chunk("Wcq")], axis=2).reshape(C, NC * 96)
    cols["wk1"] = _pad_rows(L0("Wck"))
    cols["bqkqk"] = np.concatenate([L0(n).reshape(NC, 4 * D0).T for n in ("bq", "bk", "bcq", "bck")])
    for i, p in ((0, ""), (1, "c")):
        cols[f"wv{i}"] = _pad_rows(L0(f"W{p}v"))
        cols[f"bv{i}"] = _head_vector(L0(f"b{p}v"))
    wp = np.zeros((NC, 4, 4, D0, C), np.float32)
    for j in range(4):
        wp[:, j, j] = L0("Wp").reshape(NC, 4, D0, C)[:, j]
    cols["wp"] = _chunk_rows(wp.reshape(NC * P, C))
    cols["bp"] = L0("bp")[:, None]
    cols["rw0"] = a["L0_ffn_router_W"]
    cols["rb0"] = _row_everywhere(a["L0_ffn_router_b"])
    cols["eb1"] = np.concatenate([a["L0_ffn_eb1"], a["L0_ffn_sb1"][None]]).T
    eb2 = np.zeros((P, C), np.float32)
    eb2[0:E0] = a["L0_ffn_eb2"]
    eb2[32:32 + E0] = a["L0_ffn_eb2"]
    cols["eb2"] = eb2
    cols["sb2"] = a["L0_ffn_sb2"][:, None]
    for i, p in ((2, "a1_"), (3, "a2_")):
        for n in "qkv":
            w = L1(p + "w" + n)
            cols[f"w{n}{i}"] = _pad_rows(w.transpose(1, 0, 2).reshape(w.shape[1], H * D1))
        cols[f"li1_{i}"] = _chunk_rows(L1(p + "li1_w"))
        cols[f"li2_{i}"] = L1(p + "li2_w")
        cols[f"li3_{i}"] = _chunk_rows(L1(p + "li3_w"))
        cols[f"li1b_{i}"] = L1(p + "li1_b")[:, None]
        cols[f"li2b_{i}"] = L1(p + "li2_b").reshape(NC, P).T
        cols[f"li3b_{i}"] = L1(p + "li3_b")[:, None]
        for g, n in (("x", "lnx"), ("y", "lny"), ("3", "ln3")):
            cols[f"g{g}_{i}"] = _pad_rows(L1(p + n + "_g")[:, None])
            cols[f"b{g}_{i}"] = _pad_rows(L1(p + n + "_b")[:, None])
    for n in ("ln1", "ln2"):
        cols[n + "g"] = _row_everywhere(L1(n + "_g"))
        cols[n + "b"] = _row_everywhere(L1(n + "_b"))
    cols["rw1"] = a["L1_ffn_router_w"]
    cols["rb1"] = _row_everywhere(a["L1_ffn_router_b"])
    cols["fb1"] = np.concatenate([a["L1_ffn_b1"].reshape(NR1, P), a["L1_ffn_sb1"].reshape(-1, P)]).T
    cols["fb2"] = np.concatenate([a["L1_ffn_b2"], a["L1_ffn_b2"]])
    cols["fsb2"] = a["L1_ffn_sb2"].T
    resident = np.concatenate([cols[n] for n in COLS], axis=1)
    assert resident.shape == (P, NCOLS)
    w1 = np.concatenate([a["L0_ffn_eW1"], a["L0_ffn_sW1"][None]])
    w2 = np.concatenate([a["L0_ffn_eW2"], a["L0_ffn_sW2"][None]])
    pieces0 = np.concatenate([w1, w2], axis=2).transpose(1, 0, 2)
    w1 = np.concatenate([a["L1_ffn_w1"].reshape(NR1, 4, C, 32).transpose(0, 2, 1, 3).reshape(NR1, C, P),
                         a["L1_ffn_sw1"].reshape(2, C, 2, P).transpose(0, 2, 1, 3).reshape(4, C, P)])
    w2 = np.concatenate([a["L1_ffn_w2"].reshape(NR1, P, C), a["L1_ffn_sw2"].reshape(4, P, C)])
    pieces1 = np.concatenate([w1, w2], axis=2).transpose(1, 0, 2)
    return {"in_resident": resident, "in_pieces0": pieces0, "in_pieces1": pieces1,
            "in_x": a["x"], "in_ctx": a["ctx_512"]}


def kernel(**inputs):
    import concourse.bacc as bacc
    from concourse.bass_utils import run_bass_kernel_spmd

    arrays = {n: np.ascontiguousarray(v) for n, v in lay_out({n: np.asarray(v) for n, v in inputs.items()}).items()}
    nc = bacc.Bacc("TRN2", target_bir_lowering=False, num_devices=1)
    args = [nc.dram_tensor(n, v.shape, mybir.dt.from_np(v.dtype), kind="ExternalInput").ap() for n, v in arrays.items()]
    out = nc.dram_tensor("out", (NB, S, C), F32, kind="ExternalOutput").ap()
    build(nc, *args, out)
    r = run_bass_kernel_spmd(nc, [arrays], core_ids=[0])
    return r.results[0]["out"]
```
